# Optimizing a Trainium2 kernel written in Bass

```python
import numpy as np
import jax
import jax.numpy as jnp

def _softmax(x, axis=-1):
    return jax.nn.softmax(x, axis=axis)

def _gelu(x):
    return jax.nn.gelu(x, approximate=True)

def _silu(x):
    return jax.nn.silu(x)

def _sigmoid(x):
    return jax.nn.sigmoid(x)

def _layernorm(x, axis=-1, eps=1e-05):
    m = jnp.mean(x, axis=axis, keepdims=True)
    v = jnp.var(x, axis=axis, keepdims=True)
    return (x - m) / jnp.sqrt(v + eps)

def _scatter_add(tgt, idx, src, axis=0):
    return tgt.at[idx].add(src)

def _segment_sum(src, seg, n):
    return jax.ops.segment_sum(src, seg, n)
kernel_name = 'mk_adaln_attn_ffn_d1_seqx_r4_76762b'

def setup_inputs(seed: int=0):
    np.random.seed(seed)
    _w = jnp.asarray

    def _rec_inputs():
        import jax
        import jax.numpy as jnp
        _rk = jax.random.key(seed)
        x = -7.109e-05 + 0.9999 * jax.random.normal(jax.random.fold_in(_rk, 1), (32, 64, 1024), jnp.float32)
        _lenS = 64 - jax.random.randint(jax.random.fold_in(_rk, 7), (32,), 0, max(1, 64 // 4) + 1, jnp.int32)
        _lenS2 = 64 - jax.random.randint(jax.random.fold_in(_rk, 8), (32,), 0, max(1, 64 // 4) + 1, jnp.int32)
        itok_B_0_15 = jax.random.randint(jax.random.fold_in(_rk, 11), (32,), 0, 16, jnp.int32)
        condB_coeff = 0.00219231 + 0.0100837 * jax.random.normal(jax.random.fold_in(_rk, 12), (32,), jnp.float32)
        _validS = jnp.arange(64)[None, :] < _lenS[:, None]
        _validS2 = jnp.arange(64)[None, :] < _lenS2[:, None]
        _causal = jnp.tril(jnp.ones((64, 64), dtype=bool))
        mask_Bx4096x4096_ik1 = jnp.where(jnp.ones((32, 1024, 1024), dtype=bool), 1, 0).astype(jnp.int32)
        return (x, itok_B_0_15, condB_coeff, mask_Bx4096x4096_ik1)
    x, itok_B_0_15, condB_coeff, mask_Bx4096x4096_ik1 = _rec_inputs()

    def _L0_cond_setup():
        import jax, jax.numpy as jnp
        import numpy as np
        NUM_CONDITIONS = 16
        IN_CH = 64
        OUT_CH = 64
        B = 64
        T = 1024
        key = jax.random.key(seed)
        k_x, k_w, k_c = jax.random.split(key, 3)
        x = jax.random.normal(k_x, (B, IN_CH, T), dtype=jnp.float32)
        bound = float(np.sqrt(6.0 / IN_CH))
        weights = jax.random.uniform(k_w, (NUM_CONDITIONS, IN_CH, OUT_CH), dtype=jnp.float32, minval=-bound, maxval=bound)
        condition = jax.random.randint(k_c, (B,), 0, NUM_CONDITIONS, dtype=jnp.int64)
        return {'x': x, 'weights': weights, 'condition': condition}
    _L0_cond_all = _L0_cond_setup()
    _L0_cond_in = {k: v for k, v in _L0_cond_all.items() if k in ('weights',)}
    del _L0_cond_all

    def _L0_attn_setup():
        import jax, jax.numpy as jnp
        import numpy as np
        import math
        FACTOR = 1
        key = jax.random.key(seed)
        x = jax.random.normal(key, (8, 128, 1024), dtype=jnp.float32)
        return {'x': x}
    _L0_attn_all = _L0_attn_setup()
    _L0_attn_in = {k: v for k, v in _L0_attn_all.items() if k in ()}
    del _L0_attn_all

    def _L0_cond2_setup():
        import jax, jax.numpy as jnp
        import numpy as np
        B, S, D_IN, D_OUT = (4, 128, 1024, 1024)
        key = jax.random.key(seed)
        k1, k2, k3, k4, k5 = jax.random.split(key, 5)
        hidden_states = jax.random.normal(k1, (B, S, D_IN), dtype=jnp.float32)
        W = jax.random.normal(k2, (D_OUT, D_IN), dtype=jnp.float32) * 0.02
        b = jax.random.normal(k3, (D_OUT,), dtype=jnp.float32) * 0.02
        coeff = jax.random.normal(k4, (B,), dtype=jnp.float32) * 0.01
        mask = jax.random.randint(k5, (B, D_IN, D_OUT), 0, 2, dtype=jnp.int32)
        return {'hidden_states': hidden_states, 'W': W, 'b': b, 'coeff': coeff, 'mask': mask}
    _L0_cond2_all = _L0_cond2_setup()
    _L0_cond2_in = {k: v for k, v in _L0_cond2_all.items() if k in ('W', 'b')}
    del _L0_cond2_all

    def _L0_ffn_setup():
        import jax, jax.numpy as jnp
        import numpy as np
        IN_F = 1024
        OUT_F = 1024
        B, S = (4, 512)

        def _quantize_weight(w_float):
            w_amax = jnp.abs(w_float).max()
            scale = jnp.where(w_amax == 0, 1.0, w_amax / 127.0)
            w_int8 = jnp.clip(jnp.round(w_float / scale), -127, 127).astype(jnp.int8)
            low4_amax = jnp.abs(w_int8.astype(jnp.float32)).max()
            low4_scale = jnp.where(low4_amax == 0, 1.0, low4_amax / 7.0)
            w_low = jnp.clip(jnp.round(w_int8.astype(jnp.float32) / low4_scale), -7, 7).astype(jnp.int8)
            w_rec = jnp.round(w_low.astype(jnp.float32) * low4_scale).astype(jnp.int8)
            w_high = jnp.clip(w_int8.astype(jnp.int32) - w_rec.astype(jnp.int32), -7, 7).astype(jnp.int8)
            reg_b = (w_rec.astype(jnp.int32) + w_high.astype(jnp.int32)).astype(jnp.int8)
            return (reg_b, scale.astype(jnp.float32))
        key = jax.random.key(seed)
        k1, k2, k3 = jax.random.split(key, 3)
        w_float = jax.random.normal(k1, (OUT_F, IN_F), dtype=jnp.float32) * 0.02
        reg_b, w_scale = _quantize_weight(w_float)
        x = jax.random.normal(k2, (B, S, IN_F), dtype=jnp.float32)
        bias = jax.random.normal(k3, (OUT_F,), dtype=jnp.float32) * 0.01
        return {'x': x, 'w_int': reg_b, 'w_scale': w_scale, 'bias': bias}
    _L0_ffn_all = _L0_ffn_setup()
    _L0_ffn_in = {k: v for k, v in _L0_ffn_all.items() if k in ('w_int', 'w_scale', 'bias')}
    del _L0_ffn_all
    return {'x': x, 'itok_B_0_15': itok_B_0_15, 'condB_coeff': condB_coeff, 'mask_Bx4096x4096_ik1': mask_Bx4096x4096_ik1, 'L0_cond_weights': _L0_cond_in['weights'], 'L0_cond2_W': _L0_cond2_in['W'], 'L0_cond2_b': _L0_cond2_in['b'], 'L0_ffn_w_int': _L0_ffn_in['w_int'], 'L0_ffn_w_scale': _L0_ffn_in['w_scale'], 'L0_ffn_bias': _L0_ffn_in['bias']}

def reference(x, itok_B_0_15, condB_coeff, mask_Bx4096x4096_ik1, L0_cond_weights, L0_cond2_W, L0_cond2_b, L0_ffn_w_int, L0_ffn_w_scale, L0_ffn_bias):
    import jax
    import jax.numpy as jnp

    def _L0_cond_ref(x, weights, condition):
        import jax, jax.numpy as jnp
        import numpy as np
        NUM_CONDITIONS = 16
        IN_CH = 64
        OUT_CH = 64
        B = 64
        T = 1024
        W = weights[condition]
        return jnp.einsum('bct,bcd->bdt', x, W)

    def _L0_attn_ref(x):
        import jax, jax.numpy as jnp
        import numpy as np
        import math
        FACTOR = 1
        B, C, L = x.shape
        xh = x[:, None]
        f = jnp.fft.rfft(xh, axis=-1)
        corr = jnp.fft.irfft(f * jnp.conj(f), n=L, axis=-1)
        top_k = int(FACTOR * math.log(L))
        weights, delay = jax.lax.top_k(corr, top_k)
        tmp_corr = jax.nn.softmax(weights, axis=-1)
        init_index = jnp.arange(L)
        idx = (init_index[None, None, None, None, :] + delay[..., None]) % L
        pattern = jnp.take_along_axis(xh[:, :, :, None, :], idx, axis=-1)
        delays_agg = jnp.sum(pattern * tmp_corr[..., None], axis=-2)
        return delays_agg[:, 0]

    def _L0_cond2_ref(hidden_states, W, b, coeff, mask):
        import jax, jax.numpy as jnp
        import numpy as np
        B, S, D_IN, D_OUT = (4, 128, 1024, 1024)
        output = jnp.einsum('bsi,oi->bso', hidden_states, W) + b
        sign = (2 * mask - 1).astype(hidden_states.dtype)
        diff = jnp.einsum('bsi,bio->bso', hidden_states, sign)
        return output + diff * coeff[:, None, None]

    def _L0_ffn_ref(x, w_int, w_scale, bias):
        import jax, jax.numpy as jnp
        import numpy as np
        IN_F = 1024
        OUT_F = 1024
        B, S = (4, 512)

        def _quantize_weight(w_float):
            w_amax = jnp.abs(w_float).max()
            scale = jnp.where(w_amax == 0, 1.0, w_amax / 127.0)
            w_int8 = jnp.clip(jnp.round(w_float / scale), -127, 127).astype(jnp.int8)
            low4_amax = jnp.abs(w_int8.astype(jnp.float32)).max()
            low4_scale = jnp.where(low4_amax == 0, 1.0, low4_amax / 7.0)
            w_low = jnp.clip(jnp.round(w_int8.astype(jnp.float32) / low4_scale), -7, 7).astype(jnp.int8)
            w_rec = jnp.round(w_low.astype(jnp.float32) * low4_scale).astype(jnp.int8)
            w_high = jnp.clip(w_int8.astype(jnp.int32) - w_rec.astype(jnp.int32), -7, 7).astype(jnp.int8)
            reg_b = (w_rec.astype(jnp.int32) + w_high.astype(jnp.int32)).astype(jnp.int8)
            return (reg_b, scale.astype(jnp.float32))
        x_amax = jnp.abs(x).max()
        x_scale = jnp.where(x_amax == 0, jnp.float32(1.0), x_amax / 127.0)
        x_int8 = jnp.clip(jnp.round(x / x_scale), -127, 127).astype(jnp.int8)
        out_i32 = jnp.einsum('bsk,nk->bsn', x_int8.astype(jnp.int32), w_int.astype(jnp.int32))
        combined_scale = (x_scale * w_scale).astype(jnp.bfloat16)
        out = out_i32.astype(jnp.bfloat16) * combined_scale
        out = out + bias
        return out
    x = x + _L0_attn_ref(_L0_cond_ref(x, L0_cond_weights, itok_B_0_15))
    x = x + _L0_ffn_ref(_L0_cond2_ref(x, L0_cond2_W, L0_cond2_b, condB_coeff, mask_Bx4096x4096_ik1), L0_ffn_w_int, L0_ffn_w_scale, L0_ffn_bias)
    return x

_drawn_inputs = setup_inputs


def setup_inputs(seed=0):
    import zlib

    import numpy as np

    out = dict(_drawn_inputs(seed))
    spreads = {}
    factors = {'L0_cond2_b': 3.304, 'L0_ffn_bias': 8.0}
    for name, (base, spread) in spreads.items():
        noise = np.random.default_rng([zlib.crc32(name.encode()), seed]).standard_normal(out[name].shape)
        drawn = base * np.exp(spread * noise) if base else spread * noise
        out[name] = jnp.asarray(drawn.astype(out[name].dtype))
    for name, factor in factors.items():
        out[name] = (out[name] * factor).astype(out[name].dtype)
    return out
```

```python
from contextlib import ExitStack

import numpy as np
import concourse.bass as bass
from concourse import mybir

F32 = mybir.dt.float32
F32R = mybir.dt.float32r
BF16 = mybir.dt.bfloat16
I32 = mybir.dt.int32
I8 = mybir.dt.int8
U32 = mybir.dt.uint32
ALU = mybir.AluOpType
ACT = mybir.ActivationFunctionType
AX = mybir.AxisListType

P = 128
B, C, L = 32, 64, 1024
PAIRS = B * C // P
HALF = L // 2
KC = L // P
QT = L // 4
TAU = QT + 2
TOPK = 6
NCOND = 16
MAGIC = 12582912.0
DVE_CONV, ACT_CONV = 5, 3


def transform_tables():
    t = np.arange(QT) + 0.5
    even, odd, even_s = 2 * np.arange(QT), 2 * np.arange(QT) + 1, 2 * np.arange(QT) + 2
    w = 2 * np.pi / L
    sets = [np.cos(w * np.outer(t, even)), np.cos(w * np.outer(t, odd)),
            np.sin(w * np.outer(t, even_s)), np.sin(w * np.outer(t, odd))]
    fwd = np.stack(sets).reshape(4, 2, P, QT).transpose(2, 0, 1, 3).reshape(P, KC, QT)
    tau = np.arange(QT + 1)
    inv = np.zeros((4, P, TAU))
    k_even, k_odd = even.reshape(2, P), odd.reshape(2, P)
    for c in range(2):
        inv[c, :, :QT + 1] = 2 / L * np.cos(w * np.outer(k_even[c], tau))
        inv[2 + c, :, :QT + 1] = 2 / L * np.cos(w * np.outer(k_odd[c], tau))
        inv[2 + c, :, QT] = 0.0
    inv[0, 0, :QT + 1] /= 2
    alt = np.broadcast_to((1 - 2 * (np.arange(TAU) % 2)) / L, (P, TAU)).copy()
    alt[:, QT + 1] = 0
    return (fwd.astype(np.float32), inv.transpose(1, 0, 2).copy().astype(np.float32), alt.astype(np.float32),
            np.eye(P, dtype=np.float32))


def wait(eng, sem, value):
    if not isinstance(value, int) or value > 0:
        eng.wait_ge(sem, value)


def adaln_attn_ffn(nc, x_in, itok, coeff, mask, cond_w, w2t, b2, wqt, w_scale, bias, t_fwd, t_inv, t_alt, t_eye, out):
    x_rows = x_in.rearrange("(n a) c t -> n (a c) t", a=2)
    out_rows = out.rearrange("(n a) c t -> n (a c) t", a=2)
    mask_units = mask.rearrange("b (u k p) o -> b u p k o", k=2, p=P)
    x1_dram = nc.dram_tensor("x1_scratch", (PAIRS, P, L), F32, kind="Internal").ap()
    h2_dram = nc.dram_tensor("h2_scratch", (PAIRS, P, KC, P), F32, kind="Internal").ap()

    with ExitStack() as whole:
        amax_cols = whole.enter_context(nc.sbuf_tensor("amax_cols", [P, PAIRS], F32))
        attention_and_cond(nc, x_rows, itok, coeff, mask_units, cond_w, w2t, b2, t_fwd, t_inv, t_alt, t_eye,
                           x1_dram, h2_dram, amax_cols)
        quantized_ffn(nc, wqt, w_scale, bias, x1_dram, h2_dram, amax_cols, out_rows)


def attention_and_cond(nc, x_rows, itok, coeff, mask_units, cond_w, w2t, b2, t_fwd, t_inv, t_alt, t_eye,
                       x1_dram, h2_dram, amax_cols):
    with ExitStack() as ctx:
        def sb(name, shape, dt):
            return ctx.enter_context(nc.sbuf_tensor(name, shape, dt))

        def ps(name, shape):
            return ctx.enter_context(nc.psum_tensor(name, shape, F32))

        def sem(name):
            return ctx.enter_context(nc.semaphore(name))

        w_hi, w_lo = sb("w_hi", [P, KC, L], F32R), sb("w_lo", [P, KC, L], F32R)
        fwd_hi, fwd_lo = sb("fwd_hi", [P, KC, QT], F32R), sb("fwd_lo", [P, KC, QT], F32R)
        inv_hi, inv_lo = sb("inv_hi", [P, 4, TAU], F32R), sb("inv_lo", [P, 4, TAU], F32R)
        alt = sb("alt", [P, TAU], F32)
        eye = sb("eye", [P, P], F32)
        ones = sb("ones", [P, 1], F32)
        coef = sb("coef", [P, B], F32)
        bias2 = sb("bias2", [P, KC], F32)
        tok = sb("tok", [1, B], I32)
        cond = sb("cond", [P, P], F32)
        x = [sb(f"x{q}", [P, L], F32) for q in range(2)]
        y = [sb(f"y{q}", [P, L], F32) for q in range(2)]
        fold = sb("fold", [P, 2, HALF], F32)
        fold_sum = sb("fold_sum", [P, 2, QT], F32)
        yt_hi, yt_lo = sb("yt_hi", [P, KC, P], F32R), sb("yt_lo", [P, KC, P], F32R)
        pt_hi, pt_lo = yt_hi[:, 0:4, :], yt_lo[:, 0:4, :]
        sq = sb("sq", [P, L], F32)
        ce = sb("ce", [P, TAU], F32)
        corr = sb("corr", [P, L], F32)
        top = sb("top", [P, 8], F32)
        neg_top = sb("neg_top", [P, 1], F32)
        expo = sb("expo", [P, 8], F32)
        exp_sum = sb("exp_sum", [P, 1], F32)
        off_top = sb("off_top", [P, 1], F32)
        need = sb("need", [P, 1], F32)
        flag = sb("flag", [1, 1], I32)
        prob = sb("prob", [P, 8], F32)
        lag = sb("lag", [P, 8], U32)
        bit_u = sb("bit_u", [P, 10, 8], U32)
        bit = sb("bit", [P, 10, 8], F32)
        bit_not = sb("bit_not", [P, 10, 8], F32)
        xs = [sb(f"xs{q}", [P, KC, 4, C], F32R) for q in range(2)]
        xw = sb("xw", [P, KC, P], F32R)
        mask_i = sb("mask_i", [P, KC, L], I32)
        sign = sb("sign", [P, 4, L], F32R)
        h2 = sb("h2", [P, L], F32)
        h2t = sb("h2t", [P, KC, P], F32)

        att = ps("att", [P, 2, HALF])
        turn = [ps(f"turn{h}", [P, 4, P]) for h in range(2)]
        dif = ps("dif", [P, 2, HALF])
        lin = ps("lin", [P, 2, HALF])

        const_in = sem("const_in")
        eye_in = sem("eye_in")
        table_in = [sem(f"table_in{i}") for i in range(4)]
        w_in = [sem("w_in0"), sem("w_in1")]
        x_in = [sem("x_in0"), sem("x_in1")]
        cond_in = sem("cond_in")
        mask_in = [sem(f"mask_in{u}") for u in range(4)]
        x1_stored = [sem("x1_stored0"), sem("x1_stored1")]
        h2_stored = sem("h2_stored")
        started = sem("started")
        y_mm, yt_mm, f_mm, pt_mm, corr_mm, flag_mm, xt_mm = map(
            sem, ["y_mm", "yt_mm", "f_mm", "pt_mm", "corr_mm", "flag_mm", "xt_mm"])
        sign_used, lin_mm, ht_mm = map(sem, ["sign_used", "lin_mm", "ht_mm"])
        y_sb, yt_hi_sb, sq_sb, pt_hi_sb, exp_sb, xt_hi_sb = map(
            sem, ["y_sb", "yt_hi_sb", "sq_sb", "pt_hi_sb", "exp_sb", "xt_hi_sb"])
        act_sign, dif_sb, ht_sb, table_hi_sb, w_hi_sb = map(
            sem, ["act_sign", "dif_sb", "ht_sb", "table_hi_sb", "w_hi_sb"])
        yt_lo_sb, power_sb, pt_lo_sb, ce_sb, corr_sb, top_sb = map(
            sem, ["yt_lo_sb", "power_sb", "pt_lo_sb", "ce_sb", "corr_sb", "top_sb"])
        small_sb, need_sb, flag_sb, x1_sb, xt_lo_sb = map(
            sem, ["small_sb", "need_sb", "flag_sb", "x1_sb", "xt_lo_sb"])
        dve_sign, s_sb, h2_sb, amax_sb, table_lo_sb, w_lo_sb, general, first_folds = map(
            sem, ["dve_sign", "s_sb", "h2_sb", "amax_sb", "table_lo_sb", "w_lo_sb", "general", "first_folds"])
        pool_const, fold1_sb, fold2_sb, mirror_sb, xw_sb = map(
            sem, ["pool_const", "fold1_sb", "fold2_sb", "mirror_sb", "xw_sb"])

        w_stage = mask_i[:].bitcast(F32)
        staged = [(fwd_hi[:, 0:4, :], fwd_lo[:, 0:4, :], h2[:], t_fwd[:, 0:4, :]),
                  (fwd_hi[:, 4:8, :], fwd_lo[:, 4:8, :], h2t[:].rearrange("p k r -> p (k r)"), t_fwd[:, 4:8, :]),
                  (inv_hi[:, 0:3, :], inv_lo[:, 0:3, :], corr[:, 0:3 * TAU], t_inv[:, 0:3, :]),
                  (inv_hi[:, 3:4, :], inv_lo[:, 3:4, :], ce[:], t_inv[:, 3:4, :])]

        block = ctx.enter_context(nc.Block())

        def snapped(eng, value):
            if not isinstance(value, int):
                eng.compute_val(value)
            return value

        def keep_apart(eng):
            eng.wait_ge(started, 1)

        def rows_of(b):
            return slice(C * b, C * b + C)

        def iterations(eng, body, last=1):
            body(0, 0)
            body(0, 1)
            with eng.Fori(1, PAIRS // 2 - last) as h:
                body(h, 0)
                body(h, 1)
            for h in range(PAIRS // 2 - last, PAIRS // 2):
                body(h, 0)
                body(h, 1)

        def exists(pair):
            return not isinstance(pair, int) or 0 <= pair < PAIRS

        DVE_OF = {0: [0], 1: [2], 2: [4], 3: [6, 7]}
        ACT_OF = {0: [1], 1: [3], 2: [5], 3: []}
        DVE_COUNT = {0: 1, 2: 2, 4: 3, 6: 4, 7: 5}
        ACT_COUNT = {1: 1, 3: 2, 5: 3}

        def wait_sign(eng, b, chunk):
            if chunk in DVE_COUNT:
                eng.wait_ge(dve_sign, b * DVE_CONV + DVE_COUNT[chunk])
            else:
                eng.wait_ge(act_sign, b * ACT_CONV + ACT_COUNT[chunk])

        def unit_of(p, s):
            return 2 * p + s // 4, s % 4

        @block.sync
        def _(sp):
            def load_x(pair, h, q):
                wait(sp, x1_sb, pair - 1)
                sp.dma_start(x[q][:], x_rows[pair]).then_inc(x_in[q], 16)

            def load_cond(pair):
                for b in range(2):
                    v = sp.value_load(tok[0:1, bass.ds(2 * pair + b, 1)], min_val=0, max_val=NCOND - 1)
                    if b == 0:
                        wait(sp, y_mm, pair)
                    sp.dma_start(cond[rows_of(b), rows_of(b)], cond_w[v]).then_inc(cond_in, 16)

            def load_mask(b, u):
                sp.dma_start(mask_i[:, 2 * u:2 * u + 2, :], mask_units[b, u]).then_inc(mask_in[u], 16)

            sp.dma_start(tok[:], itok.rearrange("(a n) -> a n", a=1)).then_inc(const_in, 16)
            sp.dma_start(x[0][:], x_rows[0]).then_inc(x_in[0], 16)
            sp.dma_start(eye[:], t_eye).then_inc(eye_in, 16)
            sp.wait_ge(const_in, 16)
            sp.wait_ge(pool_const, 2)
            load_cond(0)
            for i, (_, _, stage, table) in enumerate(staged):
                if i == 2:
                    sp.dma_start(x[1][:], x_rows[1]).then_inc(x_in[1], 16)
                sp.dma_start(stage, table.rearrange("p k o -> p (k o)")).then_inc(table_in[i], 16)
            load_cond(1)
            sp.dma_start(w_stage[:, 0:4, :], w2t[:, 0:4, :]).then_inc(w_in[0], 16)
            sp.dma_start(alt[:], t_alt).then_inc(const_in, 16)
            sp.dma_start(coef[:], coeff.rearrange("(a n) -> a n", a=1).broadcast_to([P, B])).then_inc(const_in, 16)
            sp.dma_start(bias2[:], b2).then_inc(const_in, 16)
            sp.dma_start(w_stage[:, 4:8, :], w2t[:, 4:8, :]).then_inc(w_in[1], 16)
            for u in range(4):
                sp.wait_ge(w_lo_sb, 2 * u + 2)
                load_mask(0, u)
                if u == 1:
                    load_cond(2)
            sp.wait_ge(dve_sign, 1)
            sp.wait_ge(act_sign, 1)
            load_mask(1, 0)
            load_x(2, 1, 0)
            sp.wait_ge(x1_sb, 1)
            sp.dma_start(x1_dram[0], y[0][:]).then_inc(x1_stored[0], 16)

            def body(h, q):
                p = 2 * h + q
                for s in range(8):
                    b, u = unit_of(p, s + 1)
                    if isinstance(b, int) and b + 1 >= B:
                        pass
                    else:
                        by_dve = snapped(sp, b * DVE_CONV + DVE_COUNT[DVE_OF[u][-1]])
                        by_act = snapped(sp, b * ACT_CONV + ACT_COUNT[ACT_OF[u][-1]]) if ACT_OF[u] else 0
                        keep_apart(sp)
                        sp.wait_ge(dve_sign, by_dve)
                        wait(sp, act_sign, by_act)
                        load_mask(b + 1, u)
                    if s == 4 and exists(p - 1):
                        wait(sp, ht_sb, p)
                        sp.dma_start(h2_dram[p - 1], h2t[:]).then_inc(h2_stored, 16)
                    if s == 3 and exists(p + 3):
                        load_cond(p + 3)
                    if s == 4 and exists(p + 3):
                        load_x(p + 3, h, 1 - q)
                    if s == 5:
                        if exists(p + 1):
                            sp.wait_ge(x1_sb, p + 2)
                            sp.dma_start(x1_dram[p + 1], y[1 - q][:]).then_inc(x1_stored[1 - q], 16)

            iterations(sp, body, last=2)
            sp.wait_ge(ht_sb, PAIRS)
            sp.dma_start(h2_dram[PAIRS - 1], h2t[:]).then_inc(h2_stored, 16)
            sp.wait_ge(h2_stored, 16 * PAIRS)
            sp.wait_ge(x1_stored[0], 16 * (PAIRS // 2))
            sp.wait_ge(x1_stored[1], 16 * (PAIRS // 2))

        @block.tensor
        def _(pe):
            def three(dst, l_hi, l_lo, r_hi, r_lo, start, stop):
                pe.matmul(dst, l_hi, r_hi, start=start, stop=False)
                pe.matmul(dst, l_hi, r_lo, start=False, stop=False)
                return pe.matmul(dst, l_lo, r_hi, start=False, stop=stop)

            def cond_y(m, h, q, dst=att):
                pe.wait_ge(x_in[q], 16 * h + 16)
                pe.wait_ge(cond_in, 32 * m + 32)
                if not isinstance(m, int) or m > 2:
                    pe.wait_ge(sq_sb, m)
                for n in range(2):
                    mm = pe.matmul(dst[:, n, :], cond[:], x[q][:, n * HALF:(n + 1) * HALF], start=True, stop=True)
                mm.then_inc(y_mm, 1)

            def transpose_y(m, waits):
                wait(pe, fold2_sb, m)
                srcs = [(fold_sum, 0), (fold, 0), (fold, 1), (fold_sum, 1)]
                for half in range(2):
                    for s, v in waits(half):
                        wait(pe, s, v)
                    for c in range(4):
                        buf, i = srcs[2 * half + c // 2]
                        mm = pe.transpose(turn[half][:, c, :], buf[:, i, (c % 2) * P:(c % 2 + 1) * P], eye[:])
                    mm.then_inc(yt_mm, 1)

            def transform(m, dst=att):
                pe.wait_ge(yt_hi_sb, 2 * m + 2)
                pe.wait_ge(yt_lo_sb, 2 * m + 2)
                for i, (bank, col) in enumerate([(0, 0), (1, 0), (0, 1), (1, 1)]):
                    for c in range(2):
                        k = 2 * i + c
                        mm = three(dst[:, bank, col * QT:(col + 1) * QT], yt_hi[:, k, :], yt_lo[:, k, :],
                                   fwd_hi[:, k, :], fwd_lo[:, k, :], c == 0, c == 1)
                mm.then_inc(f_mm, 1)

            def transpose_power(n, y_evac):
                pe.wait_ge(power_sb, n + 1)
                wait(pe, y_sb, y_evac)
                for c, at in enumerate([0, P, 2 * QT, 2 * QT + P]):
                    mm = pe.transpose(att[:, 0, c * P:(c + 1) * P], sq[:, at:at + P], eye[:])
                mm.then_inc(pt_mm, 1)

            def correlation(n):
                pe.wait_ge(pt_hi_sb, n + 1)
                pe.wait_ge(pt_lo_sb, n + 1)
                for i in range(2):
                    for c in range(2):
                        k = 2 * i + c
                        mm = three(att[:, i, 0:TAU], pt_hi[:, k, :], pt_lo[:, k, :],
                                   inv_hi[:, k, :], inv_lo[:, k, :], c == 0, c == 1)
                mm.then_inc(corr_mm, 1)

            def count_needed(n):
                pe.wait_ge(need_sb, n + 1)
                pe.matmul(att[0:1, 0, 0:1], need[:], ones[:], start=True, stop=True).then_inc(flag_mm, 1)

            def transpose_x1(n, q, after):
                pe.wait_ge(x1_sb, n + 1)
                for half in range(2):
                    wait(pe, yt_lo_sb, after + half + 1)
                    for c in range(4):
                        k = 4 * half + c
                        mm = pe.transpose(turn[half][:, c, :], y[q][:, k * P:(k + 1) * P], eye[:])
                    mm.then_inc(xt_mm, 1)

            def difference(p, q, s):
                b, u = unit_of(p, s)
                par = s // 4
                if u == 0:
                    wait(pe, s_sb, b)
                if s == 0:
                    pe.wait_ge(xt_hi_sb, 2 * p + 2)
                    pe.wait_ge(xt_lo_sb, 2 * p + 2)
                for c in (2 * u, 2 * u + 1):
                    wait_sign(pe, b, c)
                    lhs = xs[q][:, c, 2 * par:2 * par + 2, :].rearrange("p a r -> p (a r)")
                    for n in range(2):
                        mm = pe.matmul(dif[:, n, :], lhs, sign[:, c % 4, n * HALF:(n + 1) * HALF],
                                       start=(c == 0), stop=(c == KC - 1))
                    mm.then_inc(sign_used, 1)

            def linear(p, q, k):
                if k == 0:
                    wait(pe, h2_sb, p)
                    if isinstance(p, int) and p == 0:
                        pe.wait_ge(sq_sb, 2)
                        pe.wait_ge(w_hi_sb, KC)
                        pe.wait_ge(w_lo_sb, KC)
                if k % 4 == 0:
                    pe.wait_ge(xw_sb, 2 * p + k // 4 + 1)
                lo = xs[q][:, k, 1:3, :].rearrange("p a r -> p (a r)")
                for n in range(2):
                    cols = slice(n * HALF, (n + 1) * HALF)
                    mm = three(lin[:, n, :], xw[:, k, :], lo, w_hi[:, k, cols], w_lo[:, k, cols],
                               k == 0, k == KC - 1)
                if k == KC - 1:
                    mm.then_inc(lin_mm, 1)

            def transpose_h2(o):
                pe.wait_ge(h2_sb, o + 1)
                for half in range(2):
                    pe.wait_ge(xt_lo_sb, 2 * o + 2 + half + 1 if exists(o + 1) and not isinstance(o, int) else
                               min(2 * o + 2 + half + 1, 2 * PAIRS))
                    for c in range(4):
                        k = 4 * half + c
                        mm = pe.transpose(turn[half][:, c, :], h2[:, k * P:(k + 1) * P], eye[:])
                    mm.then_inc(ht_mm, 1)

            cond_y(0, 0, 0)
            pe.wait_ge(eye_in, 16)
            pe.wait_ge(first_folds, 6)
            transpose_y(0, lambda half: [])
            cond_y(1, 0, 1, lin)
            pe.wait_ge(table_hi_sb, 2)
            pe.wait_ge(table_lo_sb, 2)
            transform(0)
            transpose_power(0, 0)
            transpose_y(1, lambda half: [(yt_lo_sb, half + 1)])
            pe.wait_ge(table_hi_sb, 4)
            pe.wait_ge(table_lo_sb, 4)
            correlation(0)
            transform(1, lin)
            count_needed(0)
            transpose_x1(0, 0, 2)

            def body(h, q):
                p = 2 * h + q
                m, n, o = p + 2, p + 1, p - 1
                if exists(m):
                    cond_y(m, h + 1, q)
                difference(p, q, 0)
                if exists(n):
                    transpose_power(n, m + 1 if exists(m) else 0)
                difference(p, q, 1)
                linear(p, q, 0)
                if exists(o):
                    transpose_h2(o)
                if exists(n):
                    correlation(n)
                difference(p, q, 2)
                linear(p, q, 1)
                difference(p, q, 3)
                linear(p, q, 2)
                linear(p, q, 3)
                if exists(m):
                    if exists(o):
                        transpose_y(m, lambda half: [(ht_sb, p)])
                    else:
                        transpose_y(m, lambda half: [(xt_lo_sb, half + 1)])
                difference(p, q, 4)
                if exists(n):
                    count_needed(n)
                difference(p, q, 5)
                linear(p, q, 4)
                difference(p, q, 6)
                linear(p, q, 5)
                if exists(n):
                    if exists(m):
                        transpose_x1(n, 1 - q, 2 * m)
                    else:
                        pe.wait_ge(ht_sb, p)
                        transpose_x1(n, 1 - q, 0)
                if exists(m):
                    transform(m)
                difference(p, q, 7)
                linear(p, q, 6)
                linear(p, q, 7)

            iterations(pe, body)
            transpose_h2(PAIRS - 1)

        @block.scalar
        def _(act):
            def evac_y(m, h, q, src=att):
                act.wait_ge(y_mm, m + 1)
                wait(act, x1_stored[q], 16 * h)
                nc.scalar.activation(y[q][:].rearrange("p (n c) -> p n c", n=2), src[:], ACT.Copy).then_inc(y_sb, 1)

            def yt_high(m):
                for half in range(2):
                    act.wait_ge(yt_mm, 2 * m + half + 1)
                    nc.scalar.activation(yt_hi[:, 4 * half:4 * half + 4, :], turn[half][:], ACT.Copy)\
                        .then_inc(yt_hi_sb, 1)

            def squares(m, src=att):
                act.wait_ge(f_mm, m + 1)
                wait(act, x1_sb, m)
                nc.scalar.activation(sq[:].rearrange("p (n c) -> p n c", n=2), src[:], ACT.Square).then_inc(sq_sb, 1)

            def power_high(n):
                act.wait_ge(pt_mm, n + 1)
                nc.scalar.activation(pt_hi, att[:, 0, :].rearrange("p (c r) -> p c r", c=4), ACT.Copy)\
                    .then_inc(pt_hi_sb, 1)

            def exponentials(n):
                act.wait_ge(top_sb, 2 * n + 2)
                nc.scalar.activation(expo[:, 0:TOPK], top[:, 0:TOPK], ACT.Exp, bias=neg_top[:, 0:1],
                                     accum_out=exp_sum[:, 0:1]).then_inc(exp_sb, 1)

            def xt_high(n, q):
                for half in range(2):
                    act.wait_ge(xt_mm, 2 * n + half + 1)
                    nc.scalar.activation(xs[q][:, 4 * half:4 * half + 4, 0:4:3, :],
                                         turn[half][:].rearrange("p k (a r) -> p k a r", a=2), ACT.Copy)\
                        .then_inc(xt_hi_sb, 1)

            def convert(p, s):
                b, u = unit_of(p, s)
                if isinstance(b, int) and b >= B:
                    return
                for c in ACT_OF[u]:
                    act.wait_ge(mask_in[u], 16 * b + 16)
                    wait(act, sign_used, KC * b + c - 3)
                    nc.scalar.activation(sign[:, c % 4, :], mask_i[:, c, :], ACT.Copy, scale=2.0, bias=-1.0)\
                        .then_inc(act_sign, 1)

            def scaled_other_part(b, par, before):
                act.wait_ge(sign_used, KC * b + KC)
                wait(act, ht_mm, before)
                nc.scalar.activation(h2[rows_of(par), :].rearrange("p (n c) -> p n c", n=2), dif[rows_of(1 - par)],
                                     ACT.Copy, scale=coef[rows_of(1 - par), bass.ds(b, 1)]).then_inc(dif_sb, 1)

            def evac_h2(o):
                wait(act, h2_stored, 16 * o)
                wait(act, amax_sb, o)
                for half in range(2):
                    act.wait_ge(ht_mm, 2 * o + half + 1)
                    for c in range(4):
                        k = 4 * half + c
                        ins = nc.scalar.activation(h2t[:, k, :], turn[half][:, c, :], ACT.Identity,
                                                   bias=bias2[:, k:k + 1])
                ins.then_inc(ht_sb, 1)

            def table_high(i):
                hi, _, stage, _ = staged[i]
                act.wait_ge(table_in[i], 16)
                nc.scalar.activation(hi.rearrange("p k o -> p (k o)"), stage, ACT.Copy).then_inc(table_hi_sb, 1)

            def weights_high(k):
                act.wait_ge(w_in[k // 4], 16)
                nc.scalar.activation(w_hi[:, k, :], w_stage[:, k, :], ACT.Copy).then_inc(w_hi_sb, 1)

            evac_y(0, 0, 0)
            for i in range(4):
                table_high(i)
            yt_high(0)
            evac_y(1, 0, 1, lin)
            for k in range(0, 4):
                weights_high(k)
            squares(0)
            weights_high(4)
            power_high(0)
            weights_high(5)
            act.wait_ge(corr_mm, 1)
            yt_high(1)
            for k in range(6, 8):
                weights_high(k)
            convert(0, 0)
            act.wait_ge(const_in, 4 * 16)
            exponentials(0)
            xt_high(0, 0)
            squares(1, lin)

            def body(h, q):
                p = 2 * h + q
                m, n, o = p + 2, p + 1, p - 1
                if exists(o):
                    scaled_other_part(2 * p - 1, 1, 2 * p - 2)
                convert(p, 1)
                if exists(m):
                    evac_y(m, h + 1, q)
                convert(p, 2)
                if exists(n):
                    power_high(n)
                convert(p, 3)
                if exists(o):
                    evac_h2(o)
                convert(p, 4)
                scaled_other_part(2 * p, 0, 2 * p)
                convert(p, 5)
                if exists(n):
                    exponentials(n)
                if exists(m):
                    yt_high(m)
                convert(p, 6)
                convert(p, 7)
                if exists(n):
                    xt_high(n, 1 - q)
                convert(p, 8)
                if exists(m):
                    squares(m)

            iterations(act, body)
            scaled_other_part(2 * PAIRS - 1, 1, 2 * PAIRS - 2)
            evac_h2(PAIRS - 1)

        @block.vector
        def _(dve):
            def yt_low(m):
                for half in range(2):
                    dve.wait_ge(yt_hi_sb, 2 * m + half + 1)
                    ks = slice(4 * half, 4 * half + 4)
                    nc.vector.tensor_tensor(yt_lo[:, ks, :], turn[half][:], yt_hi[:, ks, :].bitcast(F32),
                                            ALU.subtract).then_inc(yt_lo_sb, 1)

            def power(n):
                dve.wait_ge(sq_sb, n + 1)
                nc.vector.tensor_tensor(sq[:, 1:QT], sq[:, 1:QT], sq[:, QT:2 * QT - 1], ALU.add)
                nc.vector.tensor_tensor(sq[:, 2 * QT:3 * QT], sq[:, 2 * QT:3 * QT], sq[:, 3 * QT:4 * QT], ALU.add)\
                    .then_inc(power_sb, 1)

            def power_low(n):
                dve.wait_ge(pt_hi_sb, n + 1)
                nc.vector.tensor_tensor(pt_lo, att[:, 0, :].rearrange("p (c r) -> p c r", c=4),
                                        pt_hi.bitcast(F32), ALU.subtract).then_inc(pt_lo_sb, 1)

            def correlations(n):
                dve.wait_ge(corr_mm, n + 1)
                nc.vector.scalar_tensor_tensor(out=ce[:], in0=alt[:], scalar=sq[:, 2 * QT - 1:2 * QT],
                                               in1=att[:, 0, 0:TAU], op0=ALU.mult, op1=ALU.add).then_inc(ce_sb, 1)
                dve.wait_ge(ce_sb, n + 1)
                nc.vector.tensor_tensor(corr[:, 0:QT + 1], ce[:, 0:QT + 1], att[:, 1, 0:QT + 1], ALU.add)
                nc.vector.tensor_tensor(corr[:, HALF:HALF + QT + 1], ce[:, 0:QT + 1], att[:, 1, 0:QT + 1],
                                        ALU.subtract).then_inc(corr_sb, 1)

            def top_values(n):
                made = snapped(dve, n + 1)
                keep_apart(dve)
                dve.wait_ge(mirror_sb, made)
                nc.vector.max(top[:], corr[:]).then_inc(top_sb, 1)
                dve.wait_ge(top_sb, 2 * n + 1)
                nc.vector.tensor_scalar(neg_top[:], top[:, 0:1], -1.0, None, ALU.mult).then_inc(top_sb, 1)

            def needed(n):
                nc.vector.tensor_tensor(off_top[:], top[:, 0:1], corr[:, 0:1], ALU.is_gt).then_inc(small_sb, 1)
                dve.wait_ge(small_sb, n + 1)
                dve.wait_ge(exp_sb, n + 1)
                nc.vector.scalar_tensor_tensor(out=need[:], in0=expo[:, 1:2], scalar=0.0, in1=off_top[:],
                                               op0=ALU.is_gt, op1=ALU.add).then_inc(need_sb, 1)

            def shifted_rows(q):
                done = [0]

                def step(ins):
                    done[0] += 1
                    ins.then_inc(general, 1)
                    return done[0]

                step(nc.vector.max_index(lag[:], top[:], corr[:]))
                step(nc.vector.reciprocal(exp_sum[:], exp_sum[:]))
                dve.wait_ge(general, 2)
                step(nc.vector.tensor_scalar(prob[:, 0:TOPK], expo[:, 0:TOPK], exp_sum[:, 0:1], None, ALU.mult))
                for j in range(10):
                    last = step(nc.vector.tensor_scalar(bit_u[:, j, :], lag[:], j, 1, ALU.logical_shift_right,
                                                        ALU.bitwise_and))
                dve.wait_ge(general, last)
                last = step(nc.vector.tensor_copy(bit[:], bit_u[:]))
                dve.wait_ge(general, last)
                base = step(nc.vector.tensor_scalar(bit_not[:], bit[:], -1.0, 1.0, ALU.mult, ALU.add))
                per = 3 * 10 + 1
                with dve.Fori(0, TOPK) as i:
                    src = y[q]
                    for j in range(10):
                        d, dst = 1 << j, (corr, sq)[j % 2]
                        dve.wait_ge(general, per * i + base + 3 * j)
                        nc.vector.tensor_scalar(dst[:], src[:], bit_not[:, j, bass.ds(i, 1)], None, ALU.mult)\
                            .then_inc(general, 1)
                        dve.wait_ge(general, per * i + base + 3 * j + 1)
                        for to, fr in ((slice(0, L - d), slice(d, L)), (slice(L - d, L), slice(0, d))):
                            nc.vector.scalar_tensor_tensor(out=dst[:, to], in0=src[:, fr],
                                                           scalar=bit[:, j, bass.ds(i, 1)], in1=dst[:, to],
                                                           op0=ALU.mult, op1=ALU.add).then_inc(general, 1)
                        src = dst
                    dve.wait_ge(general, per * i + base + 30)
                    nc.vector.scalar_tensor_tensor(out=x[q][:], in0=src[:], scalar=prob[:, bass.ds(i, 1)],
                                                   in1=x[q][:], op0=ALU.mult, op1=ALU.add).then_inc(general, 1)
                dve.wait_ge(general, per * TOPK + base)
                nc.vector.tensor_copy(y[q][:], x[q][:]).then_inc(general, 1)
                dve.wait_ge(general, per * TOPK + base + 1)
                dve.sem_clear(general)

            def make_x1(n, q):
                dve.wait_ge(flag_mm, n + 1)
                nc.vector.tensor_copy(flag[:], att[0:1, 0, 0:1]).then_inc(flag_sb, 1)
                made = snapped(dve, n + 1)
                keep_apart(dve)
                dve.wait_ge(flag_sb, made)
                rows = dve.value_load(flag[0:1, 0:1])
                with dve.If(rows > 0):
                    shifted_rows(q)
                with dve.Else():
                    nc.vector.tensor_tensor(y[q][:], x[q][:], y[q][:], ALU.add).then_inc(general, 1)
                    dve.wait_ge(general, 1)
                    dve.sem_clear(general)
                dve.nop().then_inc(x1_sb, 1)

            def xt_low(n, q):
                for half in range(2):
                    dve.wait_ge(xt_hi_sb, 2 * n + half + 1)
                    ks = slice(4 * half, 4 * half + 4)
                    nc.vector.tensor_tensor(xs[q][:, ks, 1:3, :],
                                            turn[half][:].rearrange("p k (a r) -> p k a r", a=2),
                                            xs[q][:, ks, 0:4:3, :].bitcast(F32), ALU.subtract).then_inc(xt_lo_sb, 1)

            def convert(p, s):
                b, u = unit_of(p, s)
                if isinstance(b, int) and b >= B:
                    return
                for c in DVE_OF[u]:
                    dve.wait_ge(mask_in[u], 16 * b + 16)
                    wait(dve, sign_used, KC * b + c - 3)
                    nc.vector.tensor_scalar(sign[:, c % 4, :], mask_i[:, c, :], 2.0, -1.0, ALU.mult, ALU.add)\
                        .then_inc(dve_sign, 1)

            def both_parts(b, par):
                dve.wait_ge(dif_sb, b + 1)
                r = rows_of(par)
                part = h2[r, :].rearrange("p (n c) -> p n c", n=2)
                nc.vector.scalar_tensor_tensor(out=part, in0=dif[r], scalar=coef[r, bass.ds(b, 1)], in1=part,
                                               op0=ALU.mult, op1=ALU.add).then_inc(s_sb, 1)

            def add_linear(o):
                dve.wait_ge(s_sb, 2 * o + 2)
                dve.wait_ge(lin_mm, o + 1)
                nc.vector.tensor_tensor(h2[:].rearrange("p (n c) -> p n c", n=2), lin[:],
                                        h2[:].rearrange("p (n c) -> p n c", n=2), ALU.add).then_inc(h2_sb, 1)

            def abs_max(o):
                dve.wait_ge(ht_sb, o + 1)
                nc.vector.tensor_reduce(amax_cols[:, bass.ds(o, 1)], h2t[:].rearrange("p k r -> p (k r)"), AX.X,
                                        ALU.max, apply_absolute_value=True).then_inc(amax_sb, 1)

            def table_low(i):
                hi, lo, stage, _ = staged[i]
                dve.wait_ge(table_hi_sb, i + 1)
                nc.vector.tensor_tensor(lo.rearrange("p k o -> p (k o)"), stage,
                                        hi.rearrange("p k o -> p (k o)").bitcast(F32), ALU.subtract)\
                    .then_inc(table_lo_sb, 1)

            def weights_low(k):
                dve.wait_ge(w_hi_sb, k + 1)
                nc.vector.tensor_tensor(w_lo[:, k, :], w_stage[:, k, :], w_hi[:, k, :].bitcast(F32),
                                        ALU.subtract).then_inc(w_lo_sb, 1)

            dve.wait_ge(y_sb, 1)
            first, last = y[0][:, 0:HALF], y[0][:, L - 1:HALF - 1:-1]
            nc.vector.tensor_tensor(fold[:, 0, :], first, last, ALU.add).then_inc(first_folds, 1)
            nc.vector.tensor_tensor(fold[:, 1, :], first, last, ALU.subtract).then_inc(first_folds, 1)
            for i in range(2):
                dve.wait_ge(first_folds, 1 + i)
                first, last = fold[:, i, 0:QT], fold[:, i, HALF - 1:QT - 1:-1]
                nc.vector.tensor_tensor(fold_sum[:, i, :], first, last, ALU.add).then_inc(first_folds, 1)
            for i in range(2):
                dve.wait_ge(first_folds, 3 + i)
                first, last = fold[:, i, 0:QT], fold[:, i, HALF - 1:QT - 1:-1]
                nc.vector.tensor_tensor(first, first, last, ALU.subtract).then_inc(first_folds, 1)
            table_low(0)
            table_low(1)
            yt_low(0)
            table_low(2)
            table_low(3)
            for k in range(0, 3):
                weights_low(k)
            power(0)
            weights_low(3)
            power_low(0)
            weights_low(4)
            dve.wait_ge(const_in, 4 * 16)
            correlations(0)
            yt_low(1)
            weights_low(5)
            top_values(0)
            weights_low(6)
            needed(0)
            weights_low(7)
            convert(0, 0)
            make_x1(0, 0)
            xt_low(0, 0)

            def body(h, q):
                p = 2 * h + q
                m, n, o = p + 2, p + 1, p - 1
                if exists(n):
                    power(n)
                if exists(o):
                    both_parts(2 * p - 1, 1)
                convert(p, 1)
                if exists(o):
                    add_linear(o)
                convert(p, 2)
                if exists(n):
                    power_low(n)
                convert(p, 3)
                if exists(n):
                    correlations(n)
                convert(p, 4)
                convert(p, 5)
                if exists(n):
                    top_values(n)
                both_parts(2 * p, 0)
                if exists(o):
                    abs_max(o)
                if exists(n):
                    needed(n)
                if exists(m):
                    yt_low(m)
                convert(p, 6)
                if exists(n):
                    make_x1(n, 1 - q)
                convert(p, 7)
                if exists(n):
                    xt_low(n, 1 - q)
                convert(p, 8)

            iterations(dve, body)
            both_parts(2 * PAIRS - 1, 1)
            add_linear(PAIRS - 1)
            abs_max(PAIRS - 1)

        @block.gpsimd
        def _(pool):
            nc.gpsimd.memset(cond[:], 0.0).then_inc(pool_const, 1)
            nc.gpsimd.memset(ones[:], 1.0).then_inc(pool_const, 1)
            pool.nop().then_inc(started, 1)

            def folds(m, q):
                pool.wait_ge(y_sb, m + 1)
                wait(pool, yt_mm, 2 * m)
                first, last = y[q][:, 0:HALF], y[q][:, L - 1:HALF - 1:-1]
                nc.gpsimd.tensor_tensor(fold[:, 0, :], first, last, ALU.add).then_inc(fold1_sb, 1)
                nc.gpsimd.tensor_tensor(fold[:, 1, :], first, last, ALU.subtract).then_inc(fold1_sb, 1)
                for i in range(2):
                    pool.wait_ge(fold1_sb, 4 * m - 2 + i)
                    first, last = fold[:, i, 0:QT], fold[:, i, HALF - 1:QT - 1:-1]
                    nc.gpsimd.tensor_tensor(fold_sum[:, i, :], first, last, ALU.add).then_inc(fold1_sb, 1)
                pool.wait_ge(fold1_sb, 4 * m)
                for i in range(2):
                    first, last = fold[:, i, 0:QT], fold[:, i, HALF - 1:QT - 1:-1]
                    ins = nc.gpsimd.tensor_tensor(first, first, last, ALU.subtract)
                ins.then_inc(fold2_sb, 1)

            def mirror(n):
                made = snapped(pool, n + 1)
                keep_apart(pool)
                pool.wait_ge(corr_sb, made)
                nc.gpsimd.tensor_copy(corr[:, QT + 1:HALF], corr[:, L - QT - 1:HALF:-1])
                nc.gpsimd.tensor_copy(corr[:, L - QT + 1:L], corr[:, QT - 1:0:-1]).then_inc(mirror_sb, 1)

            def side_by_side(p, q):
                made, used = snapped(pool, 2 * p + 2), snapped(pool, p)
                keep_apart(pool)
                pool.wait_ge(xt_hi_sb, made)
                wait(pool, lin_mm, used)
                for half in range(2):
                    ks = slice(4 * half, 4 * half + 4)
                    nc.gpsimd.tensor_copy(xw[:, ks, :].rearrange("p k (a r) -> p k a r", a=2),
                                          xs[q][:, ks, 0:4:3, :]).then_inc(xw_sb, 1)

            folds(1, 1)
            mirror(0)

            def body(h, q):
                p = 2 * h + q
                side_by_side(p, q)
                if exists(p + 2):
                    folds(p + 2, q)
                if exists(p + 1):
                    mirror(p + 1)

            iterations(pool, body)


def quantized_ffn(nc, wqt, w_scale, bias, x1_dram, h2_dram, amax_cols, out_rows):
    with ExitStack() as ctx:
        def sb(name, shape, dt):
            return ctx.enter_context(nc.sbuf_tensor(name, shape, dt))

        def sem(name):
            return ctx.enter_context(nc.semaphore(name))

        w_words = sb("w_words", [P, KC, L // 4], I32)
        w_i8 = w_words[:].bitcast(I8)
        w = sb("w_bf", [P, KC, L], BF16)
        bias_row = sb("bias_row", [P, L], F32)
        wsc = sb("wsc", [P, 1], F32)
        amax = sb("amax", [P, 1], F32)
        amax_all = sb("amax_all", [P, 1], F32)
        zero = sb("zero", [P, 1], F32)
        rest = sb("rest", [P, 1], F32)
        quot = sb("quot", [P, 1], F32)
        xsc = sb("xsc", [P, 1], F32)
        inv = sb("inv", [P, 1], F32)
        both = sb("both", [P, 1], BF16)
        both32 = sb("both32", [P, 1], F32)
        magic = sb("magic", [P, 1], F32)
        NB = 4
        h2t = sb("f_h2t", [P, NB, L], F32)
        x1 = sb("f_x1", [P, NB, L], F32)
        rnd = sb("rnd", [P, 2, L], F32)
        q8 = sb("q8", [P, 2, KC, P], BF16)
        acc = sb("acc", [P, 2, L], BF16)
        scaled = sb("scaled", [P, 2, L], BF16)
        res = sb("res", [P, NB, L], F32)
        prod = [ctx.enter_context(nc.psum_tensor(f"prod{i}", [P, 2, HALF], F32)) for i in range(2)]

        w_in, c_in = sem("f_w_in"), sem("f_c_in")
        h_in = [sem(f"f_h_in{i}") for i in range(NB)]
        x_in = [sem(f"f_x_in{i}") for i in range(NB)]
        stored = [sem(f"f_stored{i}") for i in range(NB)]
        w_bf, amax_sb, all_sb, sc_sb, magic_set, scales = map(
            sem, ["w_bf", "f_amax", "f_all", "f_sc", "f_magic", "f_scales"])
        w_act = sem("f_w_act")
        low_sb, rnd_sb, q_sb, mm_done, acc_sb, scaled_sb, xb_sb, res_sb = map(
            sem, ["f_low", "f_rnd", "f_q", "f_mm", "f_acc", "f_scaled", "f_xb", "f_res"])
        block = ctx.enter_context(nc.Block())

        def iterations(eng, body):
            for j in range(NB):
                body(0, j)
            with eng.Fori(1, PAIRS // NB) as h:
                for j in range(NB):
                    body(h, j)

        @block.sync
        def _(sp):
            sp.dma_start(w_words[:], wqt).then_inc(w_in, 16)
            sp.dma_start(wsc[:], w_scale.rearrange("(a n) -> a n", a=1).broadcast_to([P, 1])).then_inc(c_in, 16)
            sp.dma_start(bias_row[:], bias.rearrange("(a n) -> a n", a=1).broadcast_to([P, L])).then_inc(c_in, 16)

            def load(h, j):
                pair = NB * h + j
                wait(sp, rnd_sb, pair - NB + 1)
                sp.dma_start(h2t[:, j, :], h2_dram[pair].rearrange("p k r -> p (k r)")).then_inc(h_in[j], 16)
                wait(sp, res_sb, pair - NB + 1)
                sp.dma_start(x1[:, j, :], x1_dram[pair]).then_inc(x_in[j], 16)

            def store(h, j):
                pair = NB * h + j
                sp.wait_ge(res_sb, pair + 1)
                sp.dma_start(out_rows[pair], res[:, j, :]).then_inc(stored[j], 16)

            for j in range(NB):
                load(0, j)
            with sp.Fori(1, PAIRS // NB) as h:
                for j in range(NB):
                    store(h - 1, j)
                    load(h, j)
            for j in range(NB):
                store(PAIRS // NB - 1, j)
            for j in range(NB):
                sp.wait_ge(stored[j], 16 * (PAIRS // NB))

        @block.gpsimd
        def _(pool):
            nc.gpsimd.memset(magic[:], MAGIC).then_inc(magic_set, 1)
            pool.wait_ge(amax_sb, 1)
            nc.gpsimd.partition_all_reduce(amax_all[:], amax[:], P, bass.bass_isa.ReduceOp.max).then_inc(all_sb, 1)
            pool.wait_ge(c_in, 32)

            def body(h, j):
                pair = NB * h + j
                pool.wait_ge(x_in[j], 16 * h + 16)
                nc.gpsimd.tensor_tensor(x1[:, j, :], x1[:, j, :], bias_row[:], ALU.add).then_inc(xb_sb, 1)

            iterations(pool, body)

        @block.vector
        def _(dve):
            nc.vector.tensor_reduce(amax[:], amax_cols[:], AX.X, ALU.max).then_inc(amax_sb, 1)
            dve.wait_ge(w_in, 16)
            nc.vector.tensor_copy(w[:, 0:5, :], w_i8[:, 0:5, :]).then_inc(w_bf, 1)
            dve.wait_ge(all_sb, 1)
            nc.vector.tensor_scalar(zero[:], amax_all[:], 0.0, None, ALU.is_equal)
            nc.vector.tensor_scalar(quot[:], amax_all[:], 1.0 / 127.0, None, ALU.mult).then_inc(sc_sb, 1)
            dve.wait_ge(sc_sb, 1)
            nc.vector.scalar_tensor_tensor(out=rest[:], in0=quot[:], scalar=-128.0, in1=amax_all[:],
                                           op0=ALU.mult, op1=ALU.add).then_inc(sc_sb, 1)
            dve.wait_ge(sc_sb, 2)
            nc.vector.tensor_tensor(rest[:], rest[:], quot[:], ALU.add).then_inc(sc_sb, 1)
            dve.wait_ge(sc_sb, 3)
            nc.vector.scalar_tensor_tensor(out=quot[:], in0=rest[:], scalar=1.0 / 127.0, in1=quot[:],
                                           op0=ALU.mult, op1=ALU.add).then_inc(sc_sb, 1)
            dve.wait_ge(sc_sb, 4)
            nc.vector.tensor_tensor(xsc[:], quot[:], zero[:], ALU.add).then_inc(sc_sb, 1)
            dve.wait_ge(sc_sb, 5)
            nc.vector.reciprocal(inv[:], xsc[:])
            dve.wait_ge(c_in, 32)
            nc.vector.tensor_tensor(both[:], xsc[:], wsc[:], ALU.mult).then_inc(sc_sb, 1)
            dve.wait_ge(sc_sb, 6)
            nc.vector.tensor_copy(both32[:], both[:]).then_inc(scales, 1)
            dve.wait_ge(scales, 1)

            def quantize(h, j):
                pair = NB * h + j
                dve.wait_ge(rnd_sb, pair + 1)
                wait(dve, mm_done, pair - 1)
                nc.vector.tensor_scalar(rnd[:, j % 2, :], rnd[:, j % 2, :], MAGIC + 127.0, MAGIC - 127.0,
                                        ALU.min, ALU.max).then_inc(low_sb, 1)
                dve.wait_ge(low_sb, pair + 1)
                nc.vector.tensor_scalar(q8[:, j % 2].rearrange("p k r -> p (k r)"), rnd[:, j % 2, :], MAGIC, None,
                                        ALU.subtract).then_inc(q_sb, 1)

            def finish(h, j, pair):
                dve.wait_ge(acc_sb, pair + 1)
                wait(dve, res_sb, pair - 1)
                nc.vector.tensor_scalar(scaled[:, j % 2, :], acc[:, j % 2, :], both32[:, 0:1], None, ALU.mult)\
                    .then_inc(scaled_sb, 1)
                dve.wait_ge(scaled_sb, pair + 1)
                dve.wait_ge(xb_sb, pair + 1)
                wait(dve, stored[j], 16 * h)
                nc.vector.tensor_tensor(res[:, j, :], scaled[:, j % 2, :], x1[:, j, :], ALU.add).then_inc(res_sb, 1)

            for j in range(NB):
                quantize(0, j)
                if j:
                    finish(0, j - 1, j - 1)
            with dve.Fori(1, PAIRS // NB) as h:
                for j in range(NB):
                    quantize(h, j)
                    finish(h if j else h - 1, (j - 1) % NB, NB * h + j - 1)
            finish(PAIRS // NB - 1, NB - 1, PAIRS - 1)

        @block.scalar
        def _(act):
            act.wait_ge(w_in, 16)
            nc.scalar.activation(w[:, 5:8, :], w_i8[:, 5:8, :], ACT.Copy).then_inc(w_act, 1)
            act.wait_ge(scales, 1)
            act.wait_ge(magic_set, 1)

            def round_h2(h, j):
                pair = NB * h + j
                act.wait_ge(h_in[j], 16 * h + 16)
                wait(act, q_sb, pair - 1)
                nc.scalar.activation(rnd[:, j % 2, :], h2t[:, j, :], ACT.Identity, bias=magic[:, 0:1],
                                     scale=inv[:, 0:1]).then_inc(rnd_sb, 1)

            def evac(pair, j):
                act.wait_ge(mm_done, pair + 1)
                wait(act, scaled_sb, pair - 1)
                nc.scalar.activation(acc[:, j % 2, :].rearrange("p (n c) -> p n c", n=2), prod[j % 2][:], ACT.Copy)\
                    .then_inc(acc_sb, 1)

            for j in range(NB):
                round_h2(0, j)
                if j:
                    evac(j - 1, j - 1)
            with act.Fori(1, PAIRS // NB) as h:
                for j in range(NB):
                    round_h2(h, j)
                    evac(NB * h + j - 1, (j - 1) % NB)
            evac(PAIRS - 1, NB - 1)

        @block.tensor
        def _(pe):
            pe.wait_ge(w_bf, 1)
            pe.wait_ge(w_act, 1)

            def body(h, j):
                pair = NB * h + j
                pe.wait_ge(q_sb, pair + 1)
                wait(pe, acc_sb, pair - 1)
                for n in range(2):
                    for k in range(KC):
                        mm = pe.matmul(prod[j % 2][:, n, :], q8[:, j % 2, k, :], w[:, k, n * HALF:(n + 1) * HALF],
                                       start=(k == 0), stop=(k == KC - 1))
                mm.then_inc(mm_done, 1)

            iterations(pe, body)


def kernel(x, itok_B_0_15, condB_coeff, mask_Bx4096x4096_ik1, L0_cond_weights, L0_cond2_W, L0_cond2_b,
           L0_ffn_w_int, L0_ffn_w_scale, L0_ffn_bias):
    import concourse.bacc as bacc
    from concourse.bass_utils import run_bass_kernel_spmd as run

    fwd, inv, alt, eye = transform_tables()

    def rows_to_partitions(a):
        return np.ascontiguousarray(a.reshape(KC, P, L).transpose(1, 0, 2))

    arrays = {
        "x": np.ascontiguousarray(x),
        "itok": np.ascontiguousarray(itok_B_0_15),
        "coeff": np.ascontiguousarray(condB_coeff),
        "mask": np.ascontiguousarray(mask_Bx4096x4096_ik1),
        "cond_w": np.ascontiguousarray(L0_cond_weights),
        "w2t": rows_to_partitions(np.asarray(L0_cond2_W).T),
        "b2": np.ascontiguousarray(np.asarray(L0_cond2_b).reshape(KC, P).T),
        "wqt": rows_to_partitions(np.asarray(L0_ffn_w_int).T).view(np.int32),
        "w_scale": np.ascontiguousarray(np.asarray(L0_ffn_w_scale).reshape(1)),
        "bias": np.ascontiguousarray(L0_ffn_bias),
        "t_fwd": fwd, "t_inv": inv, "t_alt": alt, "t_eye": eye,
    }
    nc = bacc.Bacc("TRN2", target_bir_lowering=False, num_devices=1)
    args = [nc.dram_tensor(f"in_{k}", a.shape, mybir.dt.from_np(a.dtype), kind="ExternalInput").ap()
            for k, a in arrays.items()]
    out = nc.dram_tensor("out", (B, C, L), F32, kind="ExternalOutput").ap()
    adaln_attn_ffn(nc, *args, out)
    r = run(nc, [{f"in_{k}": a for k, a in arrays.items()}], core_ids=[0])
    return r.results[0]["out"]
```

```python
from contextlib import ExitStack

import numpy as np
import concourse.bass as bass
from concourse import mybir

F32 = mybir.dt.float32
F32R = mybir.dt.float32r
BF16 = mybir.dt.bfloat16
I32 = mybir.dt.int32
I8 = mybir.dt.int8
U32 = mybir.dt.uint32
ALU = mybir.AluOpType
ACT = mybir.ActivationFunctionType
AX = mybir.AxisListType

P = 128
B, C, L = 32, 64, 1024
PAIRS = B * C // P
HALF = L // 2
KC = L // P
QT = L // 4
TAU = QT + 2
TOPK = 6
NCOND = 16
MAGIC = 12582912.0
NB = 4
RING = 3 * NB
KEPT = PAIRS - 2
DVE_CONV, ACT_CONV = 5, 3


def transform_tables():
    t = np.arange(QT) + 0.5
    even, odd, even_s = 2 * np.arange(QT), 2 * np.arange(QT) + 1, 2 * np.arange(QT) + 2
    w = 2 * np.pi / L
    sets = [np.cos(w * np.outer(t, even)), np.cos(w * np.outer(t, odd)),
            np.sin(w * np.outer(t, even_s)), np.sin(w * np.outer(t, odd))]
    fwd = np.stack(sets).reshape(4, 2, P, QT).transpose(2, 0, 1, 3).reshape(P, KC, QT)
    tau = np.arange(QT + 1)
    inv = np.zeros((4, P, TAU))
    k_even, k_odd = even.reshape(2, P), odd.reshape(2, P)
    for c in range(2):
        inv[c, :, :QT + 1] = 2 / L * np.cos(w * np.outer(k_even[c], tau))
        inv[2 + c, :, :QT + 1] = 2 / L * np.cos(w * np.outer(k_odd[c], tau))
        inv[2 + c, :, QT] = 0.0
    inv[0, 0, :QT + 1] /= 2
    alt = np.broadcast_to((1 - 2 * (np.arange(TAU) % 2)) / L, (P, TAU)).copy()
    alt[:, QT + 1] = 0
    return (fwd.astype(np.float32), inv.transpose(1, 0, 2).copy().astype(np.float32), alt.astype(np.float32),
            np.eye(P, dtype=np.float32))


def wait(eng, sem, value):
    if not isinstance(value, int) or value > 0:
        eng.wait_ge(sem, value)


def adaln_attn_ffn(nc, x_in, itok, coeff, mask, cond_w, w2t, b2, wqt, w_scale, bias, t_fwd, t_inv, t_alt, t_eye, out):
    x_rows = x_in.rearrange("(n a) c t -> n (a c) t", a=2)
    out_rows = out.rearrange("(n a) c t -> n (a c) t", a=2)
    mask_units = mask.rearrange("b (u k p) o -> b u p k o", k=2, p=P)
    x1_dram = nc.dram_tensor("x1_scratch", (PAIRS, P, L), F32, kind="Internal").ap()
    h2_dram = nc.dram_tensor("h2_scratch", (PAIRS, P, KC, P), F32, kind="Internal").ap()

    with ExitStack() as ctx:
        place = {}

        def sb(name, shape, dt):
            place[name] = -(-nc.sbuf_base // 32) * 32
            return ctx.enter_context(nc.sbuf_tensor(name, shape, dt))

        def over(earlier, name, shape, dt):
            return nc.alloc_sbuf_tensor_at(name, shape, dt, offset=place[earlier])

        def ps(name, shape):
            return ctx.enter_context(nc.psum_tensor(name, shape, F32))

        def sem(name):
            return ctx.enter_context(nc.semaphore(name))

        mask_i = sb("mask_i", [P, KC, L], I32)
        w_hi, w_lo = sb("w_hi", [P, KC, L], F32R), sb("w_lo", [P, KC, L], F32R)
        fwd_hi, fwd_lo = sb("fwd_hi", [P, KC, QT], F32R), sb("fwd_lo", [P, KC, QT], F32R)
        inv_hi, inv_lo = sb("inv_hi", [P, 4, TAU], F32R), sb("inv_lo", [P, 4, TAU], F32R)
        alt = sb("alt", [P, TAU], F32)
        eye = sb("eye", [P, P], F32)
        ones = sb("ones", [P, 1], F32)
        coef = sb("coef", [P, B], F32)
        bias2 = sb("bias2", [P, KC], F32)
        tok = sb("tok", [1, B], I32)
        cond = sb("cond", [P, P], F32)
        x = [sb(f"x{q}", [P, L], F32) for q in range(2)]
        y = [sb(f"y{q}", [P, L], F32) for q in range(2)]
        fold = sb("fold", [P, 2, HALF], F32)
        fold_sum = sb("fold_sum", [P, 2, QT], F32)
        yt_hi, yt_lo = sb("yt_hi", [P, KC, P], F32R), sb("yt_lo", [P, KC, P], F32R)
        pt_hi, pt_lo = yt_hi[:, 0:4, :], yt_lo[:, 0:4, :]
        sq = sb("sq", [P, L], F32)
        ce = sb("ce", [P, TAU], F32)
        corr = sb("corr", [P, L], F32)
        top = sb("top", [P, 8], F32)
        neg_top = sb("neg_top", [P, 1], F32)
        expo = sb("expo", [P, 8], F32)
        exp_sum = sb("exp_sum", [P, 1], F32)
        off_top = sb("off_top", [P, 1], F32)
        need = sb("need", [P, 1], F32)
        flag = sb("flag", [1, 1], I32)
        prob = sb("prob", [P, 8], F32)
        lag = sb("lag", [P, 8], U32)
        bit_u = sb("bit_u", [P, 10, 8], U32)
        bit = sb("bit", [P, 10, 8], F32)
        bit_not = sb("bit_not", [P, 10, 8], F32)
        amax_cols = sb("amax_cols", [P, PAIRS], F32)
        xs = [sb(f"xs{q}", [P, KC, 4, C], F32R) for q in range(2)]
        xw = sb("xw", [P, KC, P], F32R)
        sign = sb("sign", [P, 4, L], F32R)
        h2 = sb("h2", [P, L], F32)
        h2t = sb("h2t", [P, KC, P], F32)

        att = ps("att", [P, 2, HALF])
        turn = [ps(f"turn{h}", [P, 4, P]) for h in range(2)]
        dif = ps("dif", [P, 2, HALF])
        lin = ps("lin", [P, 2, HALF])

        w_words = over("yt_hi", "w_words", [P, KC, L // 4], I32)
        w_i8 = w_words[:].bitcast(I8)
        w_bf = over("fwd_hi", "w_bf", [P, KC, L], BF16)
        back = over("mask_i", "back", [P, RING, 2, L], F32)
        rnd = over("xs0", "rnd", [P, 2, L], F32)
        q8 = over("fold", "q8", [P, 2, KC, P], BF16)
        acc = over("corr", "acc", [P, 2, L], BF16)
        scaled = over("sq", "scaled", [P, 2, L], BF16)
        res = over("sign", "res", [P, NB, L], F32)
        bias_row = x[0]
        prod = [att, dif]
        wsc, amax, amax_all, zero, rest, quot, xsc, inv_scale, both32, magic = (
            sb(n, [P, 1], F32) for n in ["wsc", "amax", "amax_all", "zero", "rest", "quot", "xsc", "inv_scale",
                                         "both32", "magic"])
        both = sb("both", [P, 1], BF16)

        def slot(h, j, which):
            if isinstance(h, int):
                return back[:, (NB * h + j) % RING, which, :]
            return back[:, bass.ds(NB * h + j, 1), which, :].rearrange("p a t -> p (a t)")

        def h2_of(h, j):
            if isinstance(h, int) and NB * h + j >= KEPT:
                return (x[1][:], h2t[:].rearrange("p k r -> p (k r)"))[NB * h + j - KEPT]
            return slot(h, j, 0)

        def x1_of(h, j):
            if isinstance(h, int) and NB * h + j >= KEPT:
                return y[NB * h + j - KEPT][:]
            return slot(h, j, 1)

        const_in = sem("const_in")
        eye_in = sem("eye_in")
        table_in = [sem(f"table_in{i}") for i in range(4)]
        w_in = [sem("w_in0"), sem("w_in1")]
        x_in = [sem("x_in0"), sem("x_in1")]
        cond_in = sem("cond_in")
        mask_in = [sem(f"mask_in{u}") for u in range(4)]
        x1_stored = [sem("x1_stored0"), sem("x1_stored1")]
        h2_stored = sem("h2_stored")
        started = sem("started")
        y_mm, yt_mm, f_mm, pt_mm, corr_mm, flag_mm, xt_mm = map(
            sem, ["y_mm", "yt_mm", "f_mm", "pt_mm", "corr_mm", "flag_mm", "xt_mm"])
        sign_used, lin_mm, ht_mm = map(sem, ["sign_used", "lin_mm", "ht_mm"])
        y_sb, yt_hi_sb, sq_sb, pt_hi_sb, exp_sb, xt_hi_sb = map(
            sem, ["y_sb", "yt_hi_sb", "sq_sb", "pt_hi_sb", "exp_sb", "xt_hi_sb"])
        act_sign, dif_sb, ht_sb, table_hi_sb, w_hi_sb = map(
            sem, ["act_sign", "dif_sb", "ht_sb", "table_hi_sb", "w_hi_sb"])
        yt_lo_sb, power_sb, pt_lo_sb, ce_sb, corr_sb, top_sb = map(
            sem, ["yt_lo_sb", "power_sb", "pt_lo_sb", "ce_sb", "corr_sb", "top_sb"])
        small_sb, need_sb, flag_sb, x1_sb, xt_lo_sb = map(
            sem, ["small_sb", "need_sb", "flag_sb", "x1_sb", "xt_lo_sb"])
        dve_sign, s_sb, h2_sb, amax_sb, table_lo_sb, w_lo_sb, general, first_folds = map(
            sem, ["dve_sign", "s_sb", "h2_sb", "amax_sb", "table_lo_sb", "w_lo_sb", "general", "first_folds"])
        pool_const, fold1_sb, fold2_sb, mirror_sb, xw_sb = map(
            sem, ["pool_const", "fold1_sb", "fold2_sb", "mirror_sb", "xw_sb"])
        wq_in, scale_in = sem("wq_in"), sem("scale_in")
        h2_back = [sem(f"h2_back{i}") for i in range(NB)]
        x1_back = [sem(f"x1_back{i}") for i in range(NB)]
        stored = [sem(f"stored{i}") for i in range(NB)]
        wq_act, wq_dve, amax_all_sb, amax_row_sb, sc_sb, magic_set, scales = map(
            sem, ["wq_act", "wq_dve", "amax_all_sb", "amax_row_sb", "sc_sb", "magic_set", "scales"])
        low_sb, rnd_sb, q_sb, mm_done, acc_sb, scaled_sb, xb_sb, res_sb = map(
            sem, ["low_sb", "rnd_sb", "q_sb", "mm_done", "acc_sb", "scaled_sb", "xb_sb", "res_sb"])

        w_stage = mask_i[:].bitcast(F32)
        staged = [(fwd_hi[:, 0:4, :], fwd_lo[:, 0:4, :], h2[:], t_fwd[:, 0:4, :]),
                  (fwd_hi[:, 4:8, :], fwd_lo[:, 4:8, :], h2t[:].rearrange("p k r -> p (k r)"), t_fwd[:, 4:8, :]),
                  (inv_hi[:, 0:3, :], inv_lo[:, 0:3, :], corr[:, 0:3 * TAU], t_inv[:, 0:3, :]),
                  (inv_hi[:, 3:4, :], inv_lo[:, 3:4, :], ce[:], t_inv[:, 3:4, :])]

        block = ctx.enter_context(nc.Block())

        def snapped(eng, value):
            if not isinstance(value, int):
                eng.compute_val(value)
            return value

        def keep_apart(eng):
            eng.wait_ge(started, 1)

        def rows_of(b):
            return slice(C * b, C * b + C)

        def iterations(eng, body, last=1):
            body(0, 0)
            body(0, 1)
            with eng.Fori(1, PAIRS // 2 - last) as h:
                body(h, 0)
                body(h, 1)
            for h in range(PAIRS // 2 - last, PAIRS // 2):
                body(h, 0)
                body(h, 1)

        def turns(eng, body):
            for j in range(NB):
                body(0, j)
            with eng.Fori(1, PAIRS // NB - 1) as h:
                for j in range(NB):
                    body(h, j)
            for j in range(NB):
                body(PAIRS // NB - 1, j)

        def exists(pair):
            return not isinstance(pair, int) or 0 <= pair < PAIRS

        def kept(pair):
            return isinstance(pair, int) and pair >= KEPT

        DVE_OF = {0: [0], 1: [2], 2: [4], 3: [6, 7]}
        ACT_OF = {0: [1], 1: [3], 2: [5], 3: []}
        DVE_COUNT = {0: 1, 2: 2, 4: 3, 6: 4, 7: 5}
        ACT_COUNT = {1: 1, 3: 2, 5: 3}

        def wait_sign(eng, b, chunk):
            if chunk in DVE_COUNT:
                eng.wait_ge(dve_sign, b * DVE_CONV + DVE_COUNT[chunk])
            else:
                eng.wait_ge(act_sign, b * ACT_CONV + ACT_COUNT[chunk])

        def unit_of(p, s):
            return 2 * p + s // 4, s % 4

        @block.sync
        def _(sp):
            def load_x(pair, h, q):
                wait(sp, x1_sb, pair - 1)
                sp.dma_start(x[q][:], x_rows[pair]).then_inc(x_in[q], 16)

            def load_cond(pair):
                for b in range(2):
                    v = sp.value_load(tok[0:1, bass.ds(2 * pair + b, 1)], min_val=0, max_val=NCOND - 1)
                    if b == 0:
                        wait(sp, y_mm, pair)
                    sp.dma_start(cond[rows_of(b), rows_of(b)], cond_w[v]).then_inc(cond_in, 16)

            def load_mask(b, u):
                sp.dma_start(mask_i[:, 2 * u:2 * u + 2, :], mask_units[b, u]).then_inc(mask_in[u], 16)

            sp.dma_start(tok[:], itok.rearrange("(a n) -> a n", a=1)).then_inc(const_in, 16)
            sp.dma_start(x[0][:], x_rows[0]).then_inc(x_in[0], 16)
            sp.dma_start(eye[:], t_eye).then_inc(eye_in, 16)
            sp.wait_ge(const_in, 16)
            sp.wait_ge(pool_const, 2)
            load_cond(0)
            for i, (_, _, stage, table) in enumerate(staged):
                if i == 2:
                    sp.dma_start(x[1][:], x_rows[1]).then_inc(x_in[1], 16)
                sp.dma_start(stage, table.rearrange("p k o -> p (k o)")).then_inc(table_in[i], 16)
            load_cond(1)
            sp.dma_start(w_stage[:, 0:4, :], w2t[:, 0:4, :]).then_inc(w_in[0], 16)
            sp.dma_start(alt[:], t_alt).then_inc(const_in, 16)
            sp.dma_start(coef[:], coeff.rearrange("(a n) -> a n", a=1).broadcast_to([P, B])).then_inc(const_in, 16)
            sp.dma_start(bias2[:], b2).then_inc(const_in, 16)
            sp.dma_start(w_stage[:, 4:8, :], w2t[:, 4:8, :]).then_inc(w_in[1], 16)
            for u in range(4):
                sp.wait_ge(w_lo_sb, 2 * u + 2)
                load_mask(0, u)
                if u == 1:
                    load_cond(2)
            sp.wait_ge(dve_sign, 1)
            sp.wait_ge(act_sign, 1)
            load_mask(1, 0)
            load_x(2, 1, 0)
            sp.wait_ge(x1_sb, 1)
            sp.dma_start(x1_dram[0], y[0][:]).then_inc(x1_stored[0], 16)

            def body(h, q):
                p = 2 * h + q
                for s in range(8):
                    b, u = unit_of(p, s + 1)
                    if isinstance(b, int) and b + 1 >= B:
                        pass
                    else:
                        by_dve = snapped(sp, b * DVE_CONV + DVE_COUNT[DVE_OF[u][-1]])
                        by_act = snapped(sp, b * ACT_CONV + ACT_COUNT[ACT_OF[u][-1]]) if ACT_OF[u] else 0
                        keep_apart(sp)
                        sp.wait_ge(dve_sign, by_dve)
                        wait(sp, act_sign, by_act)
                        load_mask(b + 1, u)
                    if s == 4 and exists(p - 1) and not kept(p - 1):
                        wait(sp, ht_sb, p)
                        sp.dma_start(h2_dram[p - 1], h2t[:]).then_inc(h2_stored, 16)
                    if s == 3 and exists(p + 3):
                        load_cond(p + 3)
                    if s == 4 and exists(p + 3):
                        load_x(p + 3, h, 1 - q)
                    if s == 5:
                        if exists(p + 1) and not kept(p + 1):
                            sp.wait_ge(x1_sb, p + 2)
                            sp.dma_start(x1_dram[p + 1], y[1 - q][:]).then_inc(x1_stored[1 - q], 16)
                    if s == 4 and kept(p) and q == 0:
                        sp.wait_ge(corr_mm, PAIRS)
                        sp.dma_start(w_words[:], wqt).then_inc(wq_in, 16)
                        sp.wait_ge(x1_sb, PAIRS - 1)
                        sp.dma_start(bias_row[:], bias.rearrange("(a n) -> a n", a=1).broadcast_to([P, L]))\
                            .then_inc(scale_in, 16)
                        sp.dma_start(wsc[:], w_scale.rearrange("(a n) -> a n", a=1).broadcast_to([P, 1]))\
                            .then_inc(scale_in, 16)

            iterations(sp, body, last=2)
            sp.wait_ge(h2_stored, 16 * KEPT)
            sp.wait_ge(x1_stored[0], 16 * (KEPT // 2))
            sp.wait_ge(x1_stored[1], 16 * (KEPT // 2))

            def load(h, j):
                pair = NB * h + j
                if pair >= RING:
                    sp.wait_ge(rnd_sb, pair - RING + 1)
                wait(sp, h2_back[j], 16 * h)
                sp.dma_start(slot(h, j, 0), h2_dram[pair].rearrange("p k r -> p (k r)")).then_inc(h2_back[j], 16)
                if pair >= RING:
                    sp.wait_ge(res_sb, pair - RING + 1)
                wait(sp, x1_back[j], 16 * h)
                sp.dma_start(slot(h, j, 1), x1_dram[pair]).then_inc(x1_back[j], 16)

            def store(h, j):
                pair = NB * h + j
                sp.wait_ge(res_sb, pair + 1)
                sp.dma_start(out_rows[pair], res[:, j, :]).then_inc(stored[j], 16)

            for u in range(NB):
                sp.wait_ge(dve_sign, (B - 1) * DVE_CONV + DVE_COUNT[DVE_OF[u][-1]])
                if ACT_OF[u]:
                    sp.wait_ge(act_sign, (B - 1) * ACT_CONV + ACT_COUNT[ACT_OF[u][-1]])
                load(0, u)
            sp.wait_ge(lin_mm, PAIRS)
            for j in range(NB):
                load(1, j)
            for h in range(PAIRS // NB):
                for j in range(NB):
                    store(h, j)
                    if NB * (h + 2) + j < KEPT:
                        load(h + 2, j)
            for j in range(NB):
                sp.wait_ge(stored[j], 16 * (PAIRS // NB))

        @block.tensor
        def _(pe):
            def three(dst, l_hi, l_lo, r_hi, r_lo, start, stop):
                pe.matmul(dst, l_hi, r_hi, start=start, stop=False)
                pe.matmul(dst, l_hi, r_lo, start=False, stop=False)
                return pe.matmul(dst, l_lo, r_hi, start=False, stop=stop)

            def cond_y(m, h, q, dst=att):
                pe.wait_ge(x_in[q], 16 * h + 16)
                pe.wait_ge(cond_in, 32 * m + 32)
                if not isinstance(m, int) or m > 2:
                    pe.wait_ge(sq_sb, m)
                for n in range(2):
                    mm = pe.matmul(dst[:, n, :], cond[:], x[q][:, n * HALF:(n + 1) * HALF], start=True, stop=True)
                mm.then_inc(y_mm, 1)

            def transpose_y(m, waits):
                wait(pe, fold2_sb, m)
                srcs = [(fold_sum, 0), (fold, 0), (fold, 1), (fold_sum, 1)]
                for half in range(2):
                    for s, v in waits(half):
                        wait(pe, s, v)
                    for c in range(4):
                        buf, i = srcs[2 * half + c // 2]
                        mm = pe.transpose(turn[half][:, c, :], buf[:, i, (c % 2) * P:(c % 2 + 1) * P], eye[:])
                    mm.then_inc(yt_mm, 1)

            def transform(m, dst=att):
                pe.wait_ge(yt_hi_sb, 2 * m + 2)
                pe.wait_ge(yt_lo_sb, 2 * m + 2)
                for i, (bank, col) in enumerate([(0, 0), (1, 0), (0, 1), (1, 1)]):
                    for c in range(2):
                        k = 2 * i + c
                        mm = three(dst[:, bank, col * QT:(col + 1) * QT], yt_hi[:, k, :], yt_lo[:, k, :],
                                   fwd_hi[:, k, :], fwd_lo[:, k, :], c == 0, c == 1)
                mm.then_inc(f_mm, 1)

            def transpose_power(n, y_evac):
                pe.wait_ge(power_sb, n + 1)
                wait(pe, y_sb, y_evac)
                for c, at in enumerate([0, P, 2 * QT, 2 * QT + P]):
                    mm = pe.transpose(att[:, 0, c * P:(c + 1) * P], sq[:, at:at + P], eye[:])
                mm.then_inc(pt_mm, 1)

            def correlation(n):
                pe.wait_ge(pt_hi_sb, n + 1)
                pe.wait_ge(pt_lo_sb, n + 1)
                for i in range(2):
                    for c in range(2):
                        k = 2 * i + c
                        mm = three(att[:, i, 0:TAU], pt_hi[:, k, :], pt_lo[:, k, :],
                                   inv_hi[:, k, :], inv_lo[:, k, :], c == 0, c == 1)
                mm.then_inc(corr_mm, 1)

            def count_needed(n):
                pe.wait_ge(need_sb, n + 1)
                pe.matmul(att[0:1, 0, 0:1], need[:], ones[:], start=True, stop=True).then_inc(flag_mm, 1)

            def transpose_x1(n, q, after):
                pe.wait_ge(x1_sb, n + 1)
                for half in range(2):
                    wait(pe, yt_lo_sb, after + half + 1)
                    for c in range(4):
                        k = 4 * half + c
                        mm = pe.transpose(turn[half][:, c, :], y[q][:, k * P:(k + 1) * P], eye[:])
                    mm.then_inc(xt_mm, 1)

            def difference(p, q, s):
                b, u = unit_of(p, s)
                par = s // 4
                if u == 0:
                    wait(pe, s_sb, b)
                if s == 0:
                    pe.wait_ge(xt_hi_sb, 2 * p + 2)
                    pe.wait_ge(xt_lo_sb, 2 * p + 2)
                for c in (2 * u, 2 * u + 1):
                    wait_sign(pe, b, c)
                    lhs = xs[q][:, c, 2 * par:2 * par + 2, :].rearrange("p a r -> p (a r)")
                    for n in range(2):
                        mm = pe.matmul(dif[:, n, :], lhs, sign[:, c % 4, n * HALF:(n + 1) * HALF],
                                       start=(c == 0), stop=(c == KC - 1))
                    mm.then_inc(sign_used, 1)

            def linear(p, q, k):
                if k == 0:
                    wait(pe, h2_sb, p)
                    if isinstance(p, int) and p == 0:
                        pe.wait_ge(sq_sb, 2)
                        pe.wait_ge(w_hi_sb, KC)
                        pe.wait_ge(w_lo_sb, KC)
                if k % 4 == 0:
                    pe.wait_ge(xw_sb, 2 * p + k // 4 + 1)
                lo = xs[q][:, k, 1:3, :].rearrange("p a r -> p (a r)")
                for n in range(2):
                    cols = slice(n * HALF, (n + 1) * HALF)
                    mm = three(lin[:, n, :], xw[:, k, :], lo, w_hi[:, k, cols], w_lo[:, k, cols],
                               k == 0, k == KC - 1)
                if k == KC - 1:
                    mm.then_inc(lin_mm, 1)

            def transpose_h2(o):
                pe.wait_ge(h2_sb, o + 1)
                for half in range(2):
                    pe.wait_ge(xt_lo_sb, 2 * o + 2 + half + 1 if exists(o + 1) and not isinstance(o, int) else
                               min(2 * o + 2 + half + 1, 2 * PAIRS))
                    for c in range(4):
                        k = 4 * half + c
                        mm = pe.transpose(turn[half][:, c, :], h2[:, k * P:(k + 1) * P], eye[:])
                    mm.then_inc(ht_mm, 1)

            cond_y(0, 0, 0)
            pe.wait_ge(eye_in, 16)
            pe.wait_ge(first_folds, 6)
            transpose_y(0, lambda half: [])
            cond_y(1, 0, 1, lin)
            pe.wait_ge(table_hi_sb, 2)
            pe.wait_ge(table_lo_sb, 2)
            transform(0)
            transpose_power(0, 0)
            transpose_y(1, lambda half: [(yt_lo_sb, half + 1)])
            pe.wait_ge(table_hi_sb, 4)
            pe.wait_ge(table_lo_sb, 4)
            correlation(0)
            transform(1, lin)
            count_needed(0)
            transpose_x1(0, 0, 2)

            def linear_at(p, q, s):
                chunks = {1: [0], 2: [1], 3: [2], 4: [3], 5: [4], 6: [5], 7: [6, 7]}
                if isinstance(p, int) and p == PAIRS - 1:
                    chunks = {1: [0, 1], 2: [2, 3], 3: [4, 5], 4: [6, 7]}
                for k in chunks.get(s, []):
                    linear(p, q, k)

            def body(h, q):
                p = 2 * h + q
                m, n, o = p + 2, p + 1, p - 1
                if exists(m):
                    cond_y(m, h + 1, q)
                difference(p, q, 0)
                if exists(n):
                    transpose_power(n, m + 1 if exists(m) else 0)
                difference(p, q, 1)
                linear_at(p, q, 1)
                if exists(o):
                    transpose_h2(o)
                if exists(n):
                    correlation(n)
                difference(p, q, 2)
                linear_at(p, q, 2)
                difference(p, q, 3)
                linear_at(p, q, 3)
                linear_at(p, q, 4)
                if exists(m):
                    if exists(o):
                        transpose_y(m, lambda half: [(ht_sb, p)])
                    else:
                        transpose_y(m, lambda half: [(xt_lo_sb, half + 1)])
                difference(p, q, 4)
                if exists(n):
                    count_needed(n)
                difference(p, q, 5)
                linear_at(p, q, 5)
                difference(p, q, 6)
                linear_at(p, q, 6)
                if exists(n):
                    if exists(m):
                        transpose_x1(n, 1 - q, 2 * m)
                    else:
                        pe.wait_ge(ht_sb, p)
                        transpose_x1(n, 1 - q, 0)
                if exists(m):
                    transform(m)
                difference(p, q, 7)
                linear_at(p, q, 7)

            iterations(pe, body)
            transpose_h2(PAIRS - 1)

            pe.wait_ge(wq_dve, 5)
            pe.wait_ge(wq_act, 3)

            def product(h, j):
                pair = NB * h + j
                pe.wait_ge(q_sb, pair + 1)
                wait(pe, acc_sb, pair - 1)
                for n in range(2):
                    for k in range(KC):
                        mm = pe.matmul(prod[j % 2][:, n, :], q8[:, j % 2, k, :], w_bf[:, k, n * HALF:(n + 1) * HALF],
                                       start=(k == 0), stop=(k == KC - 1))
                mm.then_inc(mm_done, 1)

            turns(pe, product)

        @block.scalar
        def _(act):
            def evac_y(m, h, q, src=att):
                act.wait_ge(y_mm, m + 1)
                wait(act, x1_stored[q], 16 * h)
                nc.scalar.activation(y[q][:].rearrange("p (n c) -> p n c", n=2), src[:], ACT.Copy).then_inc(y_sb, 1)

            def yt_high(m):
                for half in range(2):
                    act.wait_ge(yt_mm, 2 * m + half + 1)
                    nc.scalar.activation(yt_hi[:, 4 * half:4 * half + 4, :], turn[half][:], ACT.Copy)\
                        .then_inc(yt_hi_sb, 1)

            def squares(m, src=att):
                act.wait_ge(f_mm, m + 1)
                wait(act, x1_sb, m)
                nc.scalar.activation(sq[:].rearrange("p (n c) -> p n c", n=2), src[:], ACT.Square).then_inc(sq_sb, 1)

            def power_high(n):
                act.wait_ge(pt_mm, n + 1)
                nc.scalar.activation(pt_hi, att[:, 0, :].rearrange("p (c r) -> p c r", c=4), ACT.Copy)\
                    .then_inc(pt_hi_sb, 1)

            def exponentials(n):
                act.wait_ge(top_sb, 2 * n + 2)
                nc.scalar.activation(expo[:, 0:TOPK], top[:, 0:TOPK], ACT.Exp, bias=neg_top[:, 0:1],
                                     accum_out=exp_sum[:, 0:1]).then_inc(exp_sb, 1)

            def xt_high(n, q):
                for half in range(2):
                    act.wait_ge(xt_mm, 2 * n + half + 1)
                    nc.scalar.activation(xs[q][:, 4 * half:4 * half + 4, 0:4:3, :],
                                         turn[half][:].rearrange("p k (a r) -> p k a r", a=2), ACT.Copy)\
                        .then_inc(xt_hi_sb, 1)

            def convert(p, s):
                b, u = unit_of(p, s)
                if isinstance(b, int) and b >= B:
                    return
                for c in ACT_OF[u]:
                    act.wait_ge(mask_in[u], 16 * b + 16)
                    wait(act, sign_used, KC * b + c - 3)
                    nc.scalar.activation(sign[:, c % 4, :], mask_i[:, c, :], ACT.Copy, scale=2.0, bias=-1.0)\
                        .then_inc(act_sign, 1)

            def scaled_other_part(b, par, before):
                act.wait_ge(sign_used, KC * b + KC)
                wait(act, ht_mm, before)
                nc.scalar.activation(h2[rows_of(par), :].rearrange("p (n c) -> p n c", n=2), dif[rows_of(1 - par)],
                                     ACT.Copy, scale=coef[rows_of(1 - par), bass.ds(b, 1)]).then_inc(dif_sb, 1)

            def evac_h2(o):
                wait(act, h2_stored, 16 * min(o, KEPT) if isinstance(o, int) else 16 * o)
                wait(act, amax_sb, o)
                dst = h2t
                if isinstance(o, int) and o == KEPT:
                    act.wait_ge(x1_sb, PAIRS)
                    dst = x[1][:].rearrange("p (k r) -> p k r", k=KC)
                for half in range(2):
                    act.wait_ge(ht_mm, 2 * o + half + 1)
                    for c in range(4):
                        k = 4 * half + c
                        ins = nc.scalar.activation(dst[:, k, :], turn[half][:, c, :], ACT.Identity,
                                                   bias=bias2[:, k:k + 1])
                ins.then_inc(ht_sb, 1)

            def table_high(i):
                hi, _, stage, _ = staged[i]
                act.wait_ge(table_in[i], 16)
                nc.scalar.activation(hi.rearrange("p k o -> p (k o)"), stage, ACT.Copy).then_inc(table_hi_sb, 1)

            def integer_weights(p, k):
                if isinstance(p, int) and p == PAIRS - 1:
                    act.wait_ge(wq_in, 16)
                    nc.scalar.activation(w_bf[:, k, :], w_i8[:, k, :], ACT.Copy).then_inc(wq_act, 1)

            def weights_high(k):
                act.wait_ge(w_in[k // 4], 16)
                nc.scalar.activation(w_hi[:, k, :], w_stage[:, k, :], ACT.Copy).then_inc(w_hi_sb, 1)

            evac_y(0, 0, 0)
            for i in range(4):
                table_high(i)
            yt_high(0)
            evac_y(1, 0, 1, lin)
            for k in range(0, 4):
                weights_high(k)
            squares(0)
            weights_high(4)
            power_high(0)
            weights_high(5)
            act.wait_ge(corr_mm, 1)
            yt_high(1)
            for k in range(6, 8):
                weights_high(k)
            convert(0, 0)
            act.wait_ge(const_in, 4 * 16)
            exponentials(0)
            xt_high(0, 0)
            squares(1, lin)

            def body(h, q):
                p = 2 * h + q
                m, n, o = p + 2, p + 1, p - 1
                if exists(o):
                    scaled_other_part(2 * p - 1, 1, 2 * p - 2)
                convert(p, 1)
                if exists(m):
                    evac_y(m, h + 1, q)
                convert(p, 2)
                if exists(n):
                    power_high(n)
                convert(p, 3)
                if exists(o):
                    evac_h2(o)
                convert(p, 4)
                integer_weights(p, 5)
                scaled_other_part(2 * p, 0, 2 * p)
                convert(p, 5)
                integer_weights(p, 6)
                if exists(n):
                    exponentials(n)
                if exists(m):
                    yt_high(m)
                convert(p, 6)
                integer_weights(p, 7)
                convert(p, 7)
                if exists(n):
                    xt_high(n, 1 - q)
                convert(p, 8)
                if exists(m):
                    squares(m)

            iterations(act, body)
            scaled_other_part(2 * PAIRS - 1, 1, 2 * PAIRS - 2)
            evac_h2(PAIRS - 1)

            act.wait_ge(scales, 1)
            act.wait_ge(magic_set, 1)

            def round_h2(h, j):
                pair = NB * h + j
                if not kept(pair):
                    act.wait_ge(h2_back[j], 16 * h + 16)
                wait(act, q_sb, pair - 1)
                nc.scalar.activation(rnd[:, j % 2, :], h2_of(h, j), ACT.Identity, bias=magic[:, 0:1],
                                     scale=inv_scale[:, 0:1]).then_inc(rnd_sb, 1)

            def evac(pair, j):
                act.wait_ge(mm_done, pair + 1)
                wait(act, scaled_sb, pair - 1)
                nc.scalar.activation(acc[:, j % 2, :].rearrange("p (n c) -> p n c", n=2), prod[j % 2][:], ACT.Copy)\
                    .then_inc(acc_sb, 1)

            def turn_of(h, j):
                round_h2(h, j)
                if isinstance(h, int) and h == 0 and j == 0:
                    return
                evac(NB * h + j - 1, (j - 1) % NB)

            turns(act, turn_of)
            evac(PAIRS - 1, NB - 1)

        @block.vector
        def _(dve):
            def yt_low(m):
                for half in range(2):
                    dve.wait_ge(yt_hi_sb, 2 * m + half + 1)
                    ks = slice(4 * half, 4 * half + 4)
                    nc.vector.tensor_tensor(yt_lo[:, ks, :], turn[half][:], yt_hi[:, ks, :].bitcast(F32),
                                            ALU.subtract).then_inc(yt_lo_sb, 1)

            def power(n):
                dve.wait_ge(sq_sb, n + 1)
                nc.vector.tensor_tensor(sq[:, 1:QT], sq[:, 1:QT], sq[:, QT:2 * QT - 1], ALU.add)
                nc.vector.tensor_tensor(sq[:, 2 * QT:3 * QT], sq[:, 2 * QT:3 * QT], sq[:, 3 * QT:4 * QT], ALU.add)\
                    .then_inc(power_sb, 1)

            def power_low(n):
                dve.wait_ge(pt_hi_sb, n + 1)
                nc.vector.tensor_tensor(pt_lo, att[:, 0, :].rearrange("p (c r) -> p c r", c=4),
                                        pt_hi.bitcast(F32), ALU.subtract).then_inc(pt_lo_sb, 1)

            def correlations(n):
                dve.wait_ge(corr_mm, n + 1)
                nc.vector.scalar_tensor_tensor(out=ce[:], in0=alt[:], scalar=sq[:, 2 * QT - 1:2 * QT],
                                               in1=att[:, 0, 0:TAU], op0=ALU.mult, op1=ALU.add).then_inc(ce_sb, 1)
                dve.wait_ge(ce_sb, n + 1)
                nc.vector.tensor_tensor(corr[:, 0:QT + 1], ce[:, 0:QT + 1], att[:, 1, 0:QT + 1], ALU.add)
                nc.vector.tensor_tensor(corr[:, HALF:HALF + QT + 1], ce[:, 0:QT + 1], att[:, 1, 0:QT + 1],
                                        ALU.subtract).then_inc(corr_sb, 1)

            def top_values(n):
                made = snapped(dve, n + 1)
                keep_apart(dve)
                dve.wait_ge(mirror_sb, made)
                nc.vector.max(top[:], corr[:]).then_inc(top_sb, 1)
                dve.wait_ge(top_sb, 2 * n + 1)
                nc.vector.tensor_scalar(neg_top[:], top[:, 0:1], -1.0, None, ALU.mult).then_inc(top_sb, 1)

            def needed(n):
                nc.vector.tensor_tensor(off_top[:], top[:, 0:1], corr[:, 0:1], ALU.is_gt).then_inc(small_sb, 1)
                dve.wait_ge(small_sb, n + 1)
                dve.wait_ge(exp_sb, n + 1)
                nc.vector.scalar_tensor_tensor(out=need[:], in0=expo[:, 1:2], scalar=0.0, in1=off_top[:],
                                               op0=ALU.is_gt, op1=ALU.add).then_inc(need_sb, 1)

            def shifted_rows(q):
                done = [0]

                def step(ins):
                    done[0] += 1
                    ins.then_inc(general, 1)
                    return done[0]

                step(nc.vector.max_index(lag[:], top[:], corr[:]))
                step(nc.vector.reciprocal(exp_sum[:], exp_sum[:]))
                dve.wait_ge(general, 2)
                step(nc.vector.tensor_scalar(prob[:, 0:TOPK], expo[:, 0:TOPK], exp_sum[:, 0:1], None, ALU.mult))
                for j in range(10):
                    last = step(nc.vector.tensor_scalar(bit_u[:, j, :], lag[:], j, 1, ALU.logical_shift_right,
                                                        ALU.bitwise_and))
                dve.wait_ge(general, last)
                last = step(nc.vector.tensor_copy(bit[:], bit_u[:]))
                dve.wait_ge(general, last)
                base = step(nc.vector.tensor_scalar(bit_not[:], bit[:], -1.0, 1.0, ALU.mult, ALU.add))
                per = 3 * 10 + 1
                with dve.Fori(0, TOPK) as i:
                    src = y[q]
                    for j in range(10):
                        d, dst = 1 << j, (corr, sq)[j % 2]
                        dve.wait_ge(general, per * i + base + 3 * j)
                        nc.vector.tensor_scalar(dst[:], src[:], bit_not[:, j, bass.ds(i, 1)], None, ALU.mult)\
                            .then_inc(general, 1)
                        dve.wait_ge(general, per * i + base + 3 * j + 1)
                        for to, fr in ((slice(0, L - d), slice(d, L)), (slice(L - d, L), slice(0, d))):
                            nc.vector.scalar_tensor_tensor(out=dst[:, to], in0=src[:, fr],
                                                           scalar=bit[:, j, bass.ds(i, 1)], in1=dst[:, to],
                                                           op0=ALU.mult, op1=ALU.add).then_inc(general, 1)
                        src = dst
                    dve.wait_ge(general, per * i + base + 30)
                    nc.vector.scalar_tensor_tensor(out=x[q][:], in0=src[:], scalar=prob[:, bass.ds(i, 1)],
                                                   in1=x[q][:], op0=ALU.mult, op1=ALU.add).then_inc(general, 1)
                dve.wait_ge(general, per * TOPK + base)
                nc.vector.tensor_copy(y[q][:], x[q][:]).then_inc(general, 1)
                dve.wait_ge(general, per * TOPK + base + 1)
                dve.sem_clear(general)

            def make_x1(n, q):
                dve.wait_ge(flag_mm, n + 1)
                nc.vector.tensor_copy(flag[:], att[0:1, 0, 0:1]).then_inc(flag_sb, 1)
                made = snapped(dve, n + 1)
                keep_apart(dve)
                dve.wait_ge(flag_sb, made)
                rows = dve.value_load(flag[0:1, 0:1])
                with dve.If(rows > 0):
                    shifted_rows(q)
                with dve.Else():
                    nc.vector.tensor_tensor(y[q][:], x[q][:], y[q][:], ALU.add).then_inc(general, 1)
                    dve.wait_ge(general, 1)
                    dve.sem_clear(general)
                dve.nop().then_inc(x1_sb, 1)

            def xt_low(n, q):
                for half in range(2):
                    dve.wait_ge(xt_hi_sb, 2 * n + half + 1)
                    ks = slice(4 * half, 4 * half + 4)
                    nc.vector.tensor_tensor(xs[q][:, ks, 1:3, :],
                                            turn[half][:].rearrange("p k (a r) -> p k a r", a=2),
                                            xs[q][:, ks, 0:4:3, :].bitcast(F32), ALU.subtract).then_inc(xt_lo_sb, 1)

            def convert(p, s):
                b, u = unit_of(p, s)
                if isinstance(b, int) and b >= B:
                    return
                for c in DVE_OF[u]:
                    dve.wait_ge(mask_in[u], 16 * b + 16)
                    wait(dve, sign_used, KC * b + c - 3)
                    nc.vector.tensor_scalar(sign[:, c % 4, :], mask_i[:, c, :], 2.0, -1.0, ALU.mult, ALU.add)\
                        .then_inc(dve_sign, 1)

            def both_parts(b, par):
                dve.wait_ge(dif_sb, b + 1)
                r = rows_of(par)
                part = h2[r, :].rearrange("p (n c) -> p n c", n=2)
                nc.vector.scalar_tensor_tensor(out=part, in0=dif[r], scalar=coef[r, bass.ds(b, 1)], in1=part,
                                               op0=ALU.mult, op1=ALU.add).then_inc(s_sb, 1)

            def add_linear(o):
                dve.wait_ge(s_sb, 2 * o + 2)
                dve.wait_ge(lin_mm, o + 1)
                nc.vector.tensor_tensor(h2[:].rearrange("p (n c) -> p n c", n=2), lin[:],
                                        h2[:].rearrange("p (n c) -> p n c", n=2), ALU.add).then_inc(h2_sb, 1)

            def abs_max(o):
                dve.wait_ge(ht_sb, o + 1)
                src = x[1][:] if isinstance(o, int) and o == KEPT else h2t[:].rearrange("p k r -> p (k r)")
                nc.vector.tensor_reduce(amax_cols[:, bass.ds(o, 1)], src, AX.X,
                                        ALU.max, apply_absolute_value=True).then_inc(amax_sb, 1)

            def table_low(i):
                hi, lo, stage, _ = staged[i]
                dve.wait_ge(table_hi_sb, i + 1)
                nc.vector.tensor_tensor(lo.rearrange("p k o -> p (k o)"), stage,
                                        hi.rearrange("p k o -> p (k o)").bitcast(F32), ALU.subtract)\
                    .then_inc(table_lo_sb, 1)

            def integer_weights(p, k):
                if isinstance(p, int) and p == PAIRS - 1:
                    dve.wait_ge(wq_in, 16)
                    nc.vector.tensor_copy(w_bf[:, k, :], w_i8[:, k, :]).then_inc(wq_dve, 1)

            def weights_low(k):
                dve.wait_ge(w_hi_sb, k + 1)
                nc.vector.tensor_tensor(w_lo[:, k, :], w_stage[:, k, :], w_hi[:, k, :].bitcast(F32),
                                        ALU.subtract).then_inc(w_lo_sb, 1)

            dve.wait_ge(y_sb, 1)
            first, last = y[0][:, 0:HALF], y[0][:, L - 1:HALF - 1:-1]
            nc.vector.tensor_tensor(fold[:, 0, :], first, last, ALU.add).then_inc(first_folds, 1)
            nc.vector.tensor_tensor(fold[:, 1, :], first, last, ALU.subtract).then_inc(first_folds, 1)
            for i in range(2):
                dve.wait_ge(first_folds, 1 + i)
                first, last = fold[:, i, 0:QT], fold[:, i, HALF - 1:QT - 1:-1]
                nc.vector.tensor_tensor(fold_sum[:, i, :], first, last, ALU.add).then_inc(first_folds, 1)
            for i in range(2):
                dve.wait_ge(first_folds, 3 + i)
                first, last = fold[:, i, 0:QT], fold[:, i, HALF - 1:QT - 1:-1]
                nc.vector.tensor_tensor(first, first, last, ALU.subtract).then_inc(first_folds, 1)
            table_low(0)
            table_low(1)
            yt_low(0)
            table_low(2)
            table_low(3)
            for k in range(0, 3):
                weights_low(k)
            power(0)
            weights_low(3)
            power_low(0)
            weights_low(4)
            dve.wait_ge(const_in, 4 * 16)
            correlations(0)
            yt_low(1)
            weights_low(5)
            top_values(0)
            weights_low(6)
            needed(0)
            weights_low(7)
            convert(0, 0)
            make_x1(0, 0)
            xt_low(0, 0)

            def body(h, q):
                p = 2 * h + q
                m, n, o = p + 2, p + 1, p - 1
                if exists(n):
                    power(n)
                if exists(o):
                    both_parts(2 * p - 1, 1)
                convert(p, 1)
                if exists(o):
                    add_linear(o)
                convert(p, 2)
                if exists(n):
                    power_low(n)
                convert(p, 3)
                integer_weights(p, 0)
                if exists(n):
                    correlations(n)
                convert(p, 4)
                integer_weights(p, 1)
                convert(p, 5)
                integer_weights(p, 2)
                if exists(n):
                    top_values(n)
                both_parts(2 * p, 0)
                if exists(o):
                    abs_max(o)
                if exists(n):
                    needed(n)
                if exists(m):
                    yt_low(m)
                convert(p, 6)
                integer_weights(p, 3)
                if exists(n):
                    make_x1(n, 1 - q)
                convert(p, 7)
                integer_weights(p, 4)
                if exists(n):
                    xt_low(n, 1 - q)
                convert(p, 8)

            iterations(dve, body)
            both_parts(2 * PAIRS - 1, 1)
            add_linear(PAIRS - 1)
            abs_max(PAIRS - 1)

            dve.wait_ge(amax_sb, PAIRS)
            nc.vector.tensor_reduce(amax[:], amax_cols[:], AX.X, ALU.max).then_inc(amax_row_sb, 1)
            dve.wait_ge(amax_all_sb, 1)
            nc.vector.tensor_scalar(zero[:], amax_all[:], 0.0, None, ALU.is_equal)
            nc.vector.tensor_scalar(quot[:], amax_all[:], 1.0 / 127.0, None, ALU.mult).then_inc(sc_sb, 1)
            dve.wait_ge(sc_sb, 1)
            nc.vector.scalar_tensor_tensor(out=rest[:], in0=quot[:], scalar=-128.0, in1=amax_all[:],
                                           op0=ALU.mult, op1=ALU.add).then_inc(sc_sb, 1)
            dve.wait_ge(sc_sb, 2)
            nc.vector.tensor_tensor(rest[:], rest[:], quot[:], ALU.add).then_inc(sc_sb, 1)
            dve.wait_ge(sc_sb, 3)
            nc.vector.scalar_tensor_tensor(out=quot[:], in0=rest[:], scalar=1.0 / 127.0, in1=quot[:],
                                           op0=ALU.mult, op1=ALU.add).then_inc(sc_sb, 1)
            dve.wait_ge(sc_sb, 4)
            nc.vector.tensor_tensor(xsc[:], quot[:], zero[:], ALU.add).then_inc(sc_sb, 1)
            dve.wait_ge(sc_sb, 5)
            nc.vector.reciprocal(inv_scale[:], xsc[:])
            dve.wait_ge(scale_in, 32)
            nc.vector.tensor_tensor(both[:], xsc[:], wsc[:], ALU.mult).then_inc(sc_sb, 1)
            dve.wait_ge(sc_sb, 6)
            nc.vector.tensor_copy(both32[:], both[:]).then_inc(scales, 1)
            dve.wait_ge(scales, 1)

            def quantize(h, j):
                pair = NB * h + j
                dve.wait_ge(rnd_sb, pair + 1)
                wait(dve, mm_done, pair - 1)
                nc.vector.tensor_scalar(rnd[:, j % 2, :], rnd[:, j % 2, :], MAGIC + 127.0, MAGIC - 127.0,
                                        ALU.min, ALU.max).then_inc(low_sb, 1)
                dve.wait_ge(low_sb, pair + 1)
                nc.vector.tensor_scalar(q8[:, j % 2].rearrange("p k r -> p (k r)"), rnd[:, j % 2, :], MAGIC, None,
                                        ALU.subtract).then_inc(q_sb, 1)

            def finish(h, j, pair):
                dve.wait_ge(acc_sb, pair + 1)
                wait(dve, res_sb, pair - 1)
                nc.vector.tensor_scalar(scaled[:, j % 2, :], acc[:, j % 2, :], both32[:, 0:1], None, ALU.mult)\
                    .then_inc(scaled_sb, 1)
                dve.wait_ge(scaled_sb, pair + 1)
                dve.wait_ge(xb_sb, pair + 1)
                wait(dve, stored[j], 16 * h)
                nc.vector.tensor_tensor(res[:, j, :], scaled[:, j % 2, :], x1_of(h, j), ALU.add).then_inc(res_sb, 1)

            def turn_of(h, j):
                quantize(h, j)
                if isinstance(h, int) and h == 0 and j == 0:
                    return
                finish(h if j else h - 1, (j - 1) % NB, NB * h + j - 1)

            turns(dve, turn_of)
            finish(PAIRS // NB - 1, NB - 1, PAIRS - 1)

        @block.gpsimd
        def _(pool):
            nc.gpsimd.memset(cond[:], 0.0).then_inc(pool_const, 1)
            nc.gpsimd.memset(ones[:], 1.0).then_inc(pool_const, 1)
            nc.gpsimd.memset(magic[:], MAGIC).then_inc(magic_set, 1)
            pool.nop().then_inc(started, 1)

            def folds(m, q):
                pool.wait_ge(y_sb, m + 1)
                wait(pool, yt_mm, 2 * m)
                first, last = y[q][:, 0:HALF], y[q][:, L - 1:HALF - 1:-1]
                nc.gpsimd.tensor_tensor(fold[:, 0, :], first, last, ALU.add).then_inc(fold1_sb, 1)
                nc.gpsimd.tensor_tensor(fold[:, 1, :], first, last, ALU.subtract).then_inc(fold1_sb, 1)
                for i in range(2):
                    pool.wait_ge(fold1_sb, 4 * m - 2 + i)
                    first, last = fold[:, i, 0:QT], fold[:, i, HALF - 1:QT - 1:-1]
                    nc.gpsimd.tensor_tensor(fold_sum[:, i, :], first, last, ALU.add).then_inc(fold1_sb, 1)
                pool.wait_ge(fold1_sb, 4 * m)
                for i in range(2):
                    first, last = fold[:, i, 0:QT], fold[:, i, HALF - 1:QT - 1:-1]
                    ins = nc.gpsimd.tensor_tensor(first, first, last, ALU.subtract)
                ins.then_inc(fold2_sb, 1)

            def mirror(n):
                made = snapped(pool, n + 1)
                keep_apart(pool)
                pool.wait_ge(corr_sb, made)
                nc.gpsimd.tensor_copy(corr[:, QT + 1:HALF], corr[:, L - QT - 1:HALF:-1])
                nc.gpsimd.tensor_copy(corr[:, L - QT + 1:L], corr[:, QT - 1:0:-1]).then_inc(mirror_sb, 1)

            def side_by_side(p, q):
                made, used = snapped(pool, 2 * p + 2), snapped(pool, p)
                keep_apart(pool)
                pool.wait_ge(xt_hi_sb, made)
                wait(pool, lin_mm, used)
                for half in range(2):
                    ks = slice(4 * half, 4 * half + 4)
                    nc.gpsimd.tensor_copy(xw[:, ks, :].rearrange("p k (a r) -> p k a r", a=2),
                                          xs[q][:, ks, 0:4:3, :]).then_inc(xw_sb, 1)

            folds(1, 1)
            mirror(0)

            def body(h, q):
                p = 2 * h + q
                side_by_side(p, q)
                if exists(p + 2):
                    folds(p + 2, q)
                if exists(p + 1):
                    mirror(p + 1)

            iterations(pool, body)

            pool.wait_ge(amax_row_sb, 1)
            nc.gpsimd.partition_all_reduce(amax_all[:], amax[:], P, bass.bass_isa.ReduceOp.max).then_inc(amax_all_sb, 1)
            pool.wait_ge(scale_in, 32)

            def add_bias(h, j):
                pair = NB * h + j
                if not kept(pair):
                    pool.wait_ge(x1_back[j], 16 * h + 16)
                nc.gpsimd.tensor_tensor(x1_of(h, j), x1_of(h, j), bias_row[:], ALU.add).then_inc(xb_sb, 1)

            turns(pool, add_bias)



def kernel(x, itok_B_0_15, condB_coeff, mask_Bx4096x4096_ik1, L0_cond_weights, L0_cond2_W, L0_cond2_b,
           L0_ffn_w_int, L0_ffn_w_scale, L0_ffn_bias):
    import concourse.bacc as bacc
    from concourse.bass_utils import run_bass_kernel_spmd as run

    fwd, inv, alt, eye = transform_tables()

    def rows_to_partitions(a):
        return np.ascontiguousarray(a.reshape(KC, P, L).transpose(1, 0, 2))

    arrays = {
        "x": np.ascontiguousarray(x),
        "itok": np.ascontiguousarray(itok_B_0_15),
        "coeff": np.ascontiguousarray(condB_coeff),
        "mask": np.ascontiguousarray(mask_Bx4096x4096_ik1),
        "cond_w": np.ascontiguousarray(L0_cond_weights),
        "w2t": rows_to_partitions(np.asarray(L0_cond2_W).T),
        "b2": np.ascontiguousarray(np.asarray(L0_cond2_b).reshape(KC, P).T),
        "wqt": rows_to_partitions(np.asarray(L0_ffn_w_int).T).view(np.int32),
        "w_scale": np.ascontiguousarray(np.asarray(L0_ffn_w_scale).reshape(1)),
        "bias": np.ascontiguousarray(L0_ffn_bias),
        "t_fwd": fwd, "t_inv": inv, "t_alt": alt, "t_eye": eye,
    }
    nc = bacc.Bacc("TRN2", target_bir_lowering=False, num_devices=1)
    args = [nc.dram_tensor(f"in_{k}", a.shape, mybir.dt.from_np(a.dtype), kind="ExternalInput").ap()
            for k, a in arrays.items()]
    out = nc.dram_tensor("out", (B, C, L), F32, kind="ExternalOutput").ap()
    adaln_attn_ffn(nc, *args, out)
    r = run(nc, [{f"in_{k}": a for k, a in arrays.items()}], core_ids=[0])
    return r.results[0]["out"]
```

```python
from contextlib import ExitStack

import numpy as np
import concourse.bass as bass
from concourse import mybir

F32 = mybir.dt.float32
F32R = mybir.dt.float32r
BF16 = mybir.dt.bfloat16
I32 = mybir.dt.int32
I8 = mybir.dt.int8
U32 = mybir.dt.uint32
ALU = mybir.AluOpType
ACT = mybir.ActivationFunctionType
AX = mybir.AxisListType

P = 128
B, C, L = 32, 64, 1024
PAIRS = B * C // P
HALF = L // 2
KC = L // P
QT = L // 4
TAU = QT + 2
TOPK = 6
NCOND = 16
MAGIC = 12582912.0
NB = 4
RING = 3 * NB
X1_KEPT = PAIRS - 2
H2_KEPT = PAIRS - 3
DVE_CONV, ACT_CONV = 5, 3


def transform_tables():
    t = np.arange(QT) + 0.5
    even, odd, even_s = 2 * np.arange(QT), 2 * np.arange(QT) + 1, 2 * np.arange(QT) + 2
    w = 2 * np.pi / L
    sets = [np.cos(w * np.outer(t, even)), np.cos(w * np.outer(t, odd)),
            np.sin(w * np.outer(t, even_s)), np.sin(w * np.outer(t, odd))]
    fwd = np.stack(sets).reshape(4, 2, P, QT).transpose(2, 0, 1, 3).reshape(P, KC, QT)
    tau = np.arange(QT + 1)
    inv = np.zeros((4, P, TAU))
    k_even, k_odd = even.reshape(2, P), odd.reshape(2, P)
    for c in range(2):
        inv[c, :, :QT + 1] = 2 / L * np.cos(w * np.outer(k_even[c], tau))
        inv[2 + c, :, :QT + 1] = 2 / L * np.cos(w * np.outer(k_odd[c], tau))
        inv[2 + c, :, QT] = 0.0
    inv[0, 0, :QT + 1] /= 2
    alt = np.broadcast_to((1 - 2 * (np.arange(TAU) % 2)) / L, (P, TAU)).copy()
    alt[:, QT + 1] = 0
    return (fwd.astype(np.float32), inv.transpose(1, 0, 2).copy().astype(np.float32), alt.astype(np.float32),
            np.eye(P, dtype=np.float32))


def wait(eng, sem, value):
    if not isinstance(value, int) or value > 0:
        eng.wait_ge(sem, value)


def adaln_attn_ffn(nc, x_in, itok, coeff, mask, cond_w, w2t, b2, wqt, w_scale, bias, t_fwd, t_inv, t_alt, t_eye, out):
    x_rows = x_in.rearrange("(n a) c t -> n (a c) t", a=2)
    out_rows = out.rearrange("(n a) c t -> n (a c) t", a=2)
    mask_units = mask.rearrange("b (u k p) o -> b u p k o", k=2, p=P)
    x1_dram = nc.dram_tensor("x1_scratch", (PAIRS, P, L), F32, kind="Internal").ap()
    h2_dram = nc.dram_tensor("h2_scratch", (PAIRS, P, KC, P), F32, kind="Internal").ap()

    with ExitStack() as ctx:
        place = {}

        def sb(name, shape, dt):
            place[name] = -(-nc.sbuf_base // 32) * 32
            return ctx.enter_context(nc.sbuf_tensor(name, shape, dt))

        def over(earlier, name, shape, dt):
            return nc.alloc_sbuf_tensor_at(name, shape, dt, offset=place[earlier])

        def ps(name, shape):
            return ctx.enter_context(nc.psum_tensor(name, shape, F32))

        def sem(name):
            return ctx.enter_context(nc.semaphore(name))

        mask_i = sb("mask_i", [P, KC, L], I32)
        w_hi, w_lo = sb("w_hi", [P, KC, L], F32R), sb("w_lo", [P, KC, L], F32R)
        fwd_hi, fwd_lo = sb("fwd_hi", [P, KC, QT], F32R), sb("fwd_lo", [P, KC, QT], F32R)
        inv_hi, inv_lo = sb("inv_hi", [P, 4, TAU], F32R), sb("inv_lo", [P, 4, TAU], F32R)
        alt = sb("alt", [P, TAU], F32)
        eye = sb("eye", [P, P], F32)
        ones = sb("ones", [P, 1], F32)
        coef = sb("coef", [P, B], F32)
        bias2 = sb("bias2", [P, KC], F32)
        tok = sb("tok", [1, B], I32)
        cond = sb("cond", [P, P], F32)
        x = [sb(f"x{q}", [P, L], F32) for q in range(2)]
        y = [sb(f"y{q}", [P, L], F32) for q in range(2)]
        fold = sb("fold", [P, 2, HALF], F32)
        fold_sum = sb("fold_sum", [P, 2, QT], F32)
        yt_hi, yt_lo = sb("yt_hi", [P, KC, P], F32R), sb("yt_lo", [P, KC, P], F32R)
        pt_hi, pt_lo = yt_hi[:, 0:4, :], yt_lo[:, 0:4, :]
        sq = sb("sq", [P, L], F32)
        ce = sb("ce", [P, TAU], F32)
        corr = sb("corr", [P, L], F32)
        top = sb("top", [P, 8], F32)
        neg_top = sb("neg_top", [P, 1], F32)
        expo = sb("expo", [P, 8], F32)
        exp_sum = sb("exp_sum", [P, 1], F32)
        off_top = sb("off_top", [P, 1], F32)
        need = sb("need", [P, 1], F32)
        flag = sb("flag", [1, 1], I32)
        prob = sb("prob", [P, 8], F32)
        lag = sb("lag", [P, 8], U32)
        bit_u = sb("bit_u", [P, 10, 8], U32)
        bit = sb("bit", [P, 10, 8], F32)
        bit_not = sb("bit_not", [P, 10, 8], F32)
        amax_cols = sb("amax_cols", [P, PAIRS + 1], F32)
        xs = [sb(f"xs{q}", [P, KC, 4, C], F32R) for q in range(2)]
        xw = sb("xw", [P, KC, P], F32R)
        sign = sb("sign", [P, 4, L], F32R)
        h2 = sb("h2", [P, L], F32)
        h2t = sb("h2t", [P, KC, P], F32)

        att = ps("att", [P, 2, HALF])
        turn = [ps(f"turn{h}", [P, 4, P]) for h in range(2)]
        dif = ps("dif", [P, 2, HALF])
        lin = ps("lin", [P, 2, HALF])

        w_words = over("yt_hi", "w_words", [P, KC, L // 4], I32)
        w_i8 = w_words[:].bitcast(I8)
        w_bf = over("fwd_hi", "w_bf", [P, KC, L], BF16)
        back = over("mask_i", "back", [P, RING, 2, L], F32)
        rnd = over("xs0", "rnd", [P, 2, L], F32)
        q8 = over("xw", "q8", [P, 2, KC, P], BF16)
        acc = over("corr", "acc", [P, 2, L], BF16)
        scaled = over("sq", "scaled", [P, 2, L], BF16)
        res = over("sign", "res", [P, NB, L], F32)
        bias_row = x[0]
        h2_kept = [fold[:].rearrange("p n c -> p (n c)"), x[1][:], h2t[:].rearrange("p k r -> p (k r)")]
        prod = [att, dif]
        wsc, amax, amax_all, zero, rest, quot, xsc, inv_scale, both32, magic = (
            sb(n, [P, 1], F32) for n in ["wsc", "amax", "amax_all", "zero", "rest", "quot", "xsc", "inv_scale",
                                         "both32", "magic"])
        both = sb("both", [P, 1], BF16)

        def slot(h, j, which):
            if isinstance(h, int):
                return back[:, (NB * h + j) % RING, which, :]
            return back[:, bass.ds(NB * h + j, 1), which, :].rearrange("p a t -> p (a t)")

        def h2_of(h, j):
            if isinstance(h, int) and NB * h + j >= H2_KEPT:
                return h2_kept[NB * h + j - H2_KEPT]
            return slot(h, j, 0)

        def x1_of(h, j):
            if isinstance(h, int) and NB * h + j >= X1_KEPT:
                return y[NB * h + j - X1_KEPT][:]
            return slot(h, j, 1)

        const_in = sem("const_in")
        eye_in = sem("eye_in")
        table_in = [sem(f"table_in{i}") for i in range(4)]
        w_in = [sem("w_in0"), sem("w_in1")]
        x_in = [sem("x_in0"), sem("x_in1")]
        cond_in = sem("cond_in")
        mask_in = [sem(f"mask_in{u}") for u in range(4)]
        x1_stored = [sem("x1_stored0"), sem("x1_stored1")]
        h2_stored = sem("h2_stored")
        started = sem("started")
        y_mm, yt_mm, f_mm, pt_mm, corr_mm, flag_mm, xt_mm = map(
            sem, ["y_mm", "yt_mm", "f_mm", "pt_mm", "corr_mm", "flag_mm", "xt_mm"])
        sign_used, lin_mm, ht_mm = map(sem, ["sign_used", "lin_mm", "ht_mm"])
        y_sb, yt_hi_sb, sq_sb, pt_hi_sb, exp_sb, xt_hi_sb = map(
            sem, ["y_sb", "yt_hi_sb", "sq_sb", "pt_hi_sb", "exp_sb", "xt_hi_sb"])
        act_sign, dif_sb, ht_sb, table_hi_sb, w_hi_sb = map(
            sem, ["act_sign", "dif_sb", "ht_sb", "table_hi_sb", "w_hi_sb"])
        yt_lo_sb, power_sb, pt_lo_sb, ce_sb, corr_sb, top_sb = map(
            sem, ["yt_lo_sb", "power_sb", "pt_lo_sb", "ce_sb", "corr_sb", "top_sb"])
        small_sb, need_sb, flag_sb, x1_sb, xt_lo_sb = map(
            sem, ["small_sb", "need_sb", "flag_sb", "x1_sb", "xt_lo_sb"])
        dve_sign, s_sb, h2_sb, amax_sb, table_lo_sb, w_lo_sb, general, first_folds = map(
            sem, ["dve_sign", "s_sb", "h2_sb", "amax_sb", "table_lo_sb", "w_lo_sb", "general", "first_folds"])
        warm_sb = sem("warm_sb")
        first_rnd, first_low, first_q = map(sem, ["first_rnd", "first_low", "first_q"])
        last_mm, last_acc, last_scaled, last_res = map(sem, ["last_mm", "last_acc", "last_scaled", "last_res"])
        last_part_sb, last_h2_sb, last_evac_sb = map(sem, ["last_part_sb", "last_h2_sb", "last_evac_sb"])
        pool_const, fold1_sb, fold2_sb, mirror_sb, xw_sb = map(
            sem, ["pool_const", "fold1_sb", "fold2_sb", "mirror_sb", "xw_sb"])
        wq_in, scale_in = sem("wq_in"), sem("scale_in")
        h2_back = [sem(f"h2_back{i}") for i in range(NB)]
        x1_back = [sem(f"x1_back{i}") for i in range(NB)]
        stored = [sem(f"stored{i}") for i in range(NB)]
        wq_act, wq_dve, amax_all_sb, amax_row_sb, sc_sb, magic_set, scales = map(
            sem, ["wq_act", "wq_dve", "amax_all_sb", "amax_row_sb", "sc_sb", "magic_set", "scales"])
        low_sb, rnd_sb, q_sb, mm_done, acc_sb, scaled_sb, xb_sb, res_sb = map(
            sem, ["low_sb", "rnd_sb", "q_sb", "mm_done", "acc_sb", "scaled_sb", "xb_sb", "res_sb"])

        w_stage = [over("sign", "w_stage0", [P, 4, L], F32), over("xs0", "w_stage1", [P, 4, L], F32)]
        warm = over("xw", "warm", [P, HALF], BF16)
        staged = [(fwd_hi[:, 0:4, :], fwd_lo[:, 0:4, :], h2[:], t_fwd[:, 0:4, :]),
                  (fwd_hi[:, 4:8, :], fwd_lo[:, 4:8, :], h2t[:].rearrange("p k r -> p (k r)"), t_fwd[:, 4:8, :]),
                  (inv_hi[:, 0:3, :], inv_lo[:, 0:3, :], corr[:, 0:3 * TAU], t_inv[:, 0:3, :]),
                  (inv_hi[:, 3:4, :], inv_lo[:, 3:4, :], ce[:], t_inv[:, 3:4, :])]

        block = ctx.enter_context(nc.Block())

        def snapped(eng, value):
            if not isinstance(value, int):
                eng.compute_val(value)
            return value

        def keep_apart(eng):
            eng.wait_ge(started, 1)

        def rows_of(b):
            return slice(C * b, C * b + C)

        def iterations(eng, body, last=1):
            body(0, 0)
            body(0, 1)
            with eng.Fori(1, PAIRS // 2 - last) as h:
                body(h, 0)
                body(h, 1)
            for h in range(PAIRS // 2 - last, PAIRS // 2):
                body(h, 0)
                body(h, 1)

        def turns(eng, body):
            for j in range(NB):
                body(0, j)
            with eng.Fori(1, PAIRS // NB - 1) as h:
                for j in range(NB):
                    body(h, j)
            for j in range(NB):
                body(PAIRS // NB - 1, j)

        def exists(pair):
            return not isinstance(pair, int) or 0 <= pair < PAIRS

        def is_first(pair):
            return isinstance(pair, int) and pair == 0

        def kept(pair, since=X1_KEPT):
            return isinstance(pair, int) and pair >= since

        DVE_OF = {0: [0], 1: [2], 2: [4], 3: [6, 7]}
        ACT_OF = {0: [1], 1: [3], 2: [5], 3: []}
        DVE_COUNT = {0: 1, 2: 2, 4: 3, 6: 4, 7: 5}
        ACT_COUNT = {1: 1, 3: 2, 5: 3}

        def the_last(b, u):
            return isinstance(b, int) and b == B - 1 and u == 3

        def wait_sign(eng, b, chunk):
            if chunk == KC - 1 and isinstance(b, int) and b == B - 1:
                eng.wait_ge(act_sign, B * ACT_CONV + 1)
            elif chunk in DVE_COUNT:
                eng.wait_ge(dve_sign, b * DVE_CONV + DVE_COUNT[chunk])
            else:
                eng.wait_ge(act_sign, b * ACT_CONV + ACT_COUNT[chunk])

        def unit_of(p, s):
            return 2 * p + s // 4, s % 4

        @block.sync
        def _(sp):
            def load_x(pair, h, q):
                wait(sp, x1_sb, pair - 1)
                sp.dma_start(x[q][:], x_rows[pair]).then_inc(x_in[q], 16)

            def load_cond(pair):
                for b in range(2):
                    v = sp.value_load(tok[0:1, bass.ds(2 * pair + b, 1)], min_val=0, max_val=NCOND - 1)
                    if b == 0:
                        wait(sp, y_mm, pair)
                    sp.dma_start(cond[rows_of(b), rows_of(b)], cond_w[v]).then_inc(cond_in, 16)

            def load_mask(b, u):
                sp.dma_start(mask_i[:, 2 * u:2 * u + 2, :], mask_units[b, u]).then_inc(mask_in[u], 16)

            sp.dma_start(tok[:], itok.rearrange("(a n) -> a n", a=1)).then_inc(const_in, 16)
            sp.dma_start(x[0][:], x_rows[0]).then_inc(x_in[0], 16)
            sp.dma_start(eye[:], t_eye).then_inc(eye_in, 16)
            sp.wait_ge(const_in, 16)
            sp.wait_ge(pool_const, 2)
            load_cond(0)
            for i, (_, _, stage, table) in enumerate(staged):
                if i == 2:
                    sp.dma_start(x[1][:], x_rows[1]).then_inc(x_in[1], 16)
                sp.dma_start(stage, table.rearrange("p k o -> p (k o)")).then_inc(table_in[i], 16)
            load_cond(1)
            sp.dma_start(w_stage[0][:], w2t[:, 0:4, :]).then_inc(w_in[0], 16)
            sp.dma_start(alt[:], t_alt).then_inc(const_in, 16)
            sp.dma_start(coef[:], coeff.rearrange("(a n) -> a n", a=1).broadcast_to([P, B])).then_inc(const_in, 16)
            sp.dma_start(bias2[:], b2).then_inc(const_in, 16)
            sp.dma_start(w_stage[1][:], w2t[:, 4:8, :]).then_inc(w_in[1], 16)
            for u in range(4):
                load_mask(0, u)
            load_cond(2)
            sp.wait_ge(dve_sign, 1)
            sp.wait_ge(act_sign, 1)
            load_mask(1, 0)
            load_x(2, 1, 0)
            sp.dma_start(x1_dram[0], y[0][:]).then_inc(x1_stored[0], 16)

            def body(h, q):
                p = 2 * h + q
                for s in range(8):
                    b, u = unit_of(p, s + 1)
                    if isinstance(b, int) and b + 1 >= B:
                        pass
                    else:
                        by_dve = snapped(sp, b * DVE_CONV + DVE_COUNT[DVE_OF[u][-1]])
                        by_act = snapped(sp, b * ACT_CONV + ACT_COUNT[ACT_OF[u][-1]]) if ACT_OF[u] else 0
                        keep_apart(sp)
                        sp.wait_ge(dve_sign, by_dve)
                        wait(sp, act_sign, by_act)
                        load_mask(b + 1, u)
                    if s == 4 and exists(p - 1) and not kept(p - 1, H2_KEPT):
                        wait(sp, ht_sb, p)
                        sp.dma_start(h2_dram[p - 1], h2t[:]).then_inc(h2_stored, 16)
                    if s == 3 and exists(p + 3):
                        load_cond(p + 3)
                    if s == (5 if is_first(p) else 4) and exists(p + 3):
                        load_x(p + 3, h, 1 - q)
                    if s == 5:
                        if exists(p + 1) and not kept(p + 1):
                            sp.wait_ge(x1_sb, p + 2)
                            sp.dma_start(x1_dram[p + 1], y[1 - q][:]).then_inc(x1_stored[1 - q], 16)
                    if s == 4 and kept(p) and q == 0:
                        sp.wait_ge(corr_mm, PAIRS)
                        sp.dma_start(w_words[:], wqt).then_inc(wq_in, 16)
                        sp.wait_ge(x1_sb, PAIRS - 1)
                        sp.dma_start(bias_row[:], bias.rearrange("(a n) -> a n", a=1).broadcast_to([P, L]))\
                            .then_inc(scale_in, 16)
                        sp.dma_start(wsc[:], w_scale.rearrange("(a n) -> a n", a=1).broadcast_to([P, 1]))\
                            .then_inc(scale_in, 16)

            iterations(sp, body, last=2)
            sp.wait_ge(h2_stored, 16 * H2_KEPT)
            sp.wait_ge(x1_stored[0], 16 * (X1_KEPT // 2))
            sp.wait_ge(x1_stored[1], 16 * (X1_KEPT // 2))

            def load(h, j):
                pair = NB * h + j
                if pair >= RING:
                    sp.wait_ge(rnd_sb, pair - RING + 1)
                if pair < H2_KEPT:
                    wait(sp, h2_back[j], 16 * h)
                    sp.dma_start(slot(h, j, 0), h2_dram[pair].rearrange("p k r -> p (k r)")).then_inc(h2_back[j], 16)
                if pair >= RING:
                    sp.wait_ge(res_sb, pair - RING + 1)
                wait(sp, x1_back[j], 16 * h)
                sp.dma_start(slot(h, j, 1), x1_dram[pair]).then_inc(x1_back[j], 16)

            def store(h, j):
                pair = NB * h + j
                sp.wait_ge(res_sb, pair + 1)
                sp.dma_start(out_rows[pair], res[:, j, :]).then_inc(stored[j], 16)

            for u in range(NB):
                sp.wait_ge(dve_sign, (B - 1) * DVE_CONV + min(u + 1, DVE_CONV - 1))
                sp.wait_ge(act_sign, (B - 1) * ACT_CONV + u + 1)
                load(0, u)
            sp.wait_ge(lin_mm, PAIRS)
            for j in range(NB):
                load(1, j)
            for h in range(PAIRS // NB):
                for j in range(NB):
                    if NB * h + j == PAIRS - 1:
                        for n in range(2):
                            cols = slice(n * HALF, (n + 1) * HALF)
                            sp.wait_ge(last_res, n + 1)
                            sp.dma_start(out_rows[PAIRS - 1][:, cols], res[:, j, cols]).then_inc(stored[j], 16)
                        continue
                    store(h, j)
                    if NB * (h + 2) + j < X1_KEPT:
                        load(h + 2, j)
            for j in range(NB):
                sp.wait_ge(stored[j], 16 * (PAIRS // NB + (j == NB - 1)))

        @block.tensor
        def _(pe):
            def three(dst, l_hi, l_lo, r_hi, r_lo, start, stop):
                pe.matmul(dst, l_hi, r_hi, start=start, stop=False)
                pe.matmul(dst, l_hi, r_lo, start=False, stop=False)
                return pe.matmul(dst, l_lo, r_hi, start=False, stop=stop)

            def cond_y(m, h, q, dst=att):
                pe.wait_ge(x_in[q], 16 * h + 16)
                pe.wait_ge(cond_in, 32 * m + 32)
                if not isinstance(m, int) or m > 2:
                    pe.wait_ge(sq_sb, m)
                for n in range(2):
                    mm = pe.matmul(dst[:, n, :], cond[:], x[q][:, n * HALF:(n + 1) * HALF], start=True, stop=True)
                mm.then_inc(y_mm, 1)

            def transpose_y(m, waits):
                wait(pe, fold2_sb, m)
                srcs = [(fold_sum, 0), (fold, 0), (fold, 1), (fold_sum, 1)]
                for half in range(2):
                    for s, v in waits(half):
                        wait(pe, s, v)
                    for c in range(4):
                        buf, i = srcs[2 * half + c // 2]
                        mm = pe.transpose(turn[half][:, c, :], buf[:, i, (c % 2) * P:(c % 2 + 1) * P], eye[:])
                    mm.then_inc(yt_mm, 1)

            def transform(m, dst=att, sets=range(4)):
                pe.wait_ge(yt_hi_sb, 2 * m + 2)
                pe.wait_ge(yt_lo_sb, 2 * m + 2)
                for i in sets:
                    bank, col = i % 2, i // 2
                    for c in range(2):
                        k = 2 * i + c
                        mm = three(dst[:, bank, col * QT:(col + 1) * QT], yt_hi[:, k, :], yt_lo[:, k, :],
                                   fwd_hi[:, k, :], fwd_lo[:, k, :], c == 0, c == 1)
                if 3 in sets:
                    mm.then_inc(f_mm, 1)

            def transpose_power(n, y_evac):
                pe.wait_ge(power_sb, n + 1)
                wait(pe, y_sb, y_evac)
                for c, at in enumerate([0, P, 2 * QT, 2 * QT + P]):
                    mm = pe.transpose(att[:, 0, c * P:(c + 1) * P], sq[:, at:at + P], eye[:])
                mm.then_inc(pt_mm, 1)

            def correlation(n):
                pe.wait_ge(pt_hi_sb, n + 1)
                pe.wait_ge(pt_lo_sb, n + 1)
                for i in range(2):
                    for c in range(2):
                        k = 2 * i + c
                        mm = three(att[:, i, 0:TAU], pt_hi[:, k, :], pt_lo[:, k, :],
                                   inv_hi[:, k, :], inv_lo[:, k, :], c == 0, c == 1)
                mm.then_inc(corr_mm, 1)

            def count_needed(n):
                pe.wait_ge(need_sb, n + 1)
                pe.matmul(att[0:1, 0, 0:1], need[:], ones[:], start=True, stop=True).then_inc(flag_mm, 1)

            def transpose_x1(n, q, after):
                pe.wait_ge(x1_sb, n + 1)
                for half in range(2):
                    wait(pe, yt_lo_sb, after + half + 1)
                    for c in range(4):
                        k = 4 * half + c
                        mm = pe.transpose(turn[half][:, c, :], y[q][:, k * P:(k + 1) * P], eye[:])
                    mm.then_inc(xt_mm, 1)

            def difference(p, q, s):
                b, u = unit_of(p, s)
                par = s // 4
                if u == 0:
                    wait(pe, s_sb, b)
                if s == 0:
                    pe.wait_ge(xt_hi_sb, 2 * p + 2)
                    pe.wait_ge(xt_lo_sb, 2 * p + 2)
                for c in (2 * u, 2 * u + 1):
                    wait_sign(pe, b, c)
                    lhs = xs[q][:, c, 2 * par:2 * par + 2, :].rearrange("p a r -> p (a r)")
                    for n in range(2):
                        mm = pe.matmul(dif[:, n, :], lhs, sign[:, c % 4, n * HALF:(n + 1) * HALF],
                                       start=(c == 0), stop=(c == KC - 1))
                    mm.then_inc(sign_used, 1)

            def linear(p, q, k):
                if k == 0:
                    wait(pe, h2_sb, p)
                    if isinstance(p, int) and p == 0:
                        pe.wait_ge(sq_sb, 2)
                        pe.wait_ge(w_hi_sb, KC)
                        pe.wait_ge(w_lo_sb, KC)
                if k % 4 == 0:
                    pe.wait_ge(xw_sb, 2 * p + k // 4 + 1)
                lo = xs[q][:, k, 1:3, :].rearrange("p a r -> p (a r)")
                for n in range(2):
                    cols = slice(n * HALF, (n + 1) * HALF)
                    mm = three(lin[:, n, :], xw[:, k, :], lo, w_hi[:, k, cols], w_lo[:, k, cols],
                               k == 0, k == KC - 1)
                if k == KC - 1:
                    mm.then_inc(lin_mm, 1)

            def transpose_h2(o):
                pe.wait_ge(h2_sb, o + 1)
                for half in range(2):
                    pe.wait_ge(xt_lo_sb, 2 * o + 3 + half)
                    for c in range(4):
                        k = 4 * half + c
                        mm = pe.transpose(turn[half][:, c, :], h2[:, k * P:(k + 1) * P], eye[:])
                    mm.then_inc(ht_mm, 1)

            def keep_warm(count, idle=warm[:], dst=dif):
                for _ in range(count):
                    pe.matmul(dst[:, 0, :], idle[:, 0:P], idle, start=True, stop=True)

            pe.wait_ge(warm_sb, 1)
            keep_warm(14)
            cond_y(0, 0, 0)
            keep_warm(10)
            pe.wait_ge(eye_in, 16)
            pe.wait_ge(first_folds, 6)
            transpose_y(0, lambda half: [])
            keep_warm(3)
            pe.wait_ge(table_hi_sb, 2)
            pe.wait_ge(table_lo_sb, 2)
            transform(0)
            cond_y(1, 0, 1, lin)
            transpose_power(0, 0)
            keep_warm(4)
            pe.wait_ge(table_hi_sb, 4)
            pe.wait_ge(table_lo_sb, 4)
            correlation(0)
            keep_warm(4)
            transpose_y(1, lambda half: [(yt_lo_sb, half + 1)])
            keep_warm(4)
            transform(1, lin, [0, 1])
            keep_warm(3)
            count_needed(0)
            transform(1, lin, [2, 3])
            keep_warm(3)
            transpose_x1(0, 0, 2)
            pe.wait_ge(w_hi_sb, 1)
            keep_warm(4, w_hi[:, 0, 0:HALF])

            def linear_at(p, q, s):
                chunks = {1: [0], 2: [1], 3: [2], 4: [3], 5: [4], 6: [5], 7: [6, 7]}
                if isinstance(p, int) and p == PAIRS - 1:
                    chunks = {1: [0, 1], 2: [2, 3], 3: [4, 5], 4: [6, 7]}
                for k in chunks.get(s, []):
                    linear(p, q, k)

            def body(h, q):
                p = 2 * h + q
                m, n, o = p + 2, p + 1, p - 1
                if isinstance(p, int) and p == 0:
                    difference(p, q, 0)
                    difference(p, q, 1)
                    cond_y(m, h + 1, q)
                    transpose_power(n, m + 1)
                else:
                    if exists(m):
                        cond_y(m, h + 1, q)
                    difference(p, q, 0)
                    if exists(n):
                        transpose_power(n, m + 1 if exists(m) else 0)
                    difference(p, q, 1)
                linear_at(p, q, 1)
                if exists(o):
                    transpose_h2(o)
                if exists(n):
                    correlation(n)
                difference(p, q, 2)
                linear_at(p, q, 2)
                difference(p, q, 3)
                linear_at(p, q, 3)
                linear_at(p, q, 4)
                if exists(m):
                    if exists(o):
                        transpose_y(m, lambda half: [(ht_sb, p)])
                    else:
                        transpose_y(m, lambda half: [(xt_lo_sb, half + 1)])
                difference(p, q, 4)
                if exists(n):
                    count_needed(n)
                difference(p, q, 5)
                linear_at(p, q, 5)
                difference(p, q, 6)
                linear_at(p, q, 6)
                if exists(n):
                    if exists(m):
                        transpose_x1(n, 1 - q, 2 * m)
                    else:
                        pe.wait_ge(ht_sb, p)
                        transpose_x1(n, 1 - q, 0)
                if exists(m):
                    transform(m)
                difference(p, q, 7)
                linear_at(p, q, 7)

            iterations(pe, body)
            pe.wait_ge(wq_dve, 1)
            keep_warm(8, w_bf[:, 0, 0:HALF], att)
            for half in range(2):
                pe.wait_ge(last_h2_sb, 2 * half + 2)
                for c in range(4):
                    k = 4 * half + c
                    mm = pe.transpose(turn[half][:, c, :], h2[:, k * P:(k + 1) * P], eye[:])
                mm.then_inc(ht_mm, 1)
            keep_warm(28, w_bf[:, 0, 0:HALF], att)

            pe.wait_ge(wq_dve, 5)
            pe.wait_ge(wq_act, 3)

            def product(h, j):
                pair = NB * h + j
                if isinstance(pair, int) and pair == 0:
                    for k in range(KC):
                        pe.wait_ge(q_sb if k >= KC // 2 else first_q, 1)
                        for n in range(2):
                            mm = pe.matmul(prod[0][:, n, :], q8[:, 0, k, :], w_bf[:, k, n * HALF:(n + 1) * HALF],
                                           start=(k == 0), stop=(k == KC - 1))
                    mm.then_inc(mm_done, 1)
                    return
                pe.wait_ge(q_sb, pair + 1)
                wait(pe, acc_sb, pair - 1)
                for n in range(2):
                    for k in range(KC):
                        mm = pe.matmul(prod[j % 2][:, n, :], q8[:, j % 2, k, :], w_bf[:, k, n * HALF:(n + 1) * HALF],
                                       start=(k == 0), stop=(k == KC - 1))
                    if isinstance(pair, int) and pair == PAIRS - 1:
                        mm.then_inc(last_mm, 1)
                if not (isinstance(pair, int) and pair == PAIRS - 1):
                    mm.then_inc(mm_done, 1)

            turns(pe, product)

        @block.scalar
        def _(act):
            def evac_y(m, h, q, src=att):
                act.wait_ge(y_mm, m + 1)
                wait(act, x1_stored[q], 16 * h)
                nc.scalar.activation(y[q][:].rearrange("p (n c) -> p n c", n=2), src[:], ACT.Copy).then_inc(y_sb, 1)

            def yt_high(m):
                for half in range(2):
                    act.wait_ge(yt_mm, 2 * m + half + 1)
                    nc.scalar.activation(yt_hi[:, 4 * half:4 * half + 4, :], turn[half][:], ACT.Copy)\
                        .then_inc(yt_hi_sb, 1)

            def squares(m, src=att):
                act.wait_ge(f_mm, m + 1)
                wait(act, x1_sb, m)
                nc.scalar.activation(sq[:].rearrange("p (n c) -> p n c", n=2), src[:], ACT.Square).then_inc(sq_sb, 1)

            def power_high(n):
                act.wait_ge(pt_mm, n + 1)
                nc.scalar.activation(pt_hi, att[:, 0, :].rearrange("p (c r) -> p c r", c=4), ACT.Copy)\
                    .then_inc(pt_hi_sb, 1)

            def exponentials(n):
                act.wait_ge(top_sb, 2 * n + 2)
                nc.scalar.activation(expo[:, 0:TOPK], top[:, 0:TOPK], ACT.Exp, bias=neg_top[:, 0:1],
                                     accum_out=exp_sum[:, 0:1]).then_inc(exp_sb, 1)

            def xt_high(n, q):
                for half in range(2):
                    act.wait_ge(xt_mm, 2 * n + half + 1)
                    nc.scalar.activation(xs[q][:, 4 * half:4 * half + 4, 0:4:3, :],
                                         turn[half][:].rearrange("p k (a r) -> p k a r", a=2), ACT.Copy)\
                        .then_inc(xt_hi_sb, 1)

            def convert(p, s):
                b, u = unit_of(p, s)
                if isinstance(b, int) and b >= B:
                    return
                for c in ACT_OF[u] if not the_last(b, u) else [KC - 1]:
                    act.wait_ge(mask_in[u], 16 * b + 16)
                    wait(act, sign_used, KC * b + c - 3)
                    nc.scalar.activation(sign[:, c % 4, :], mask_i[:, c, :], ACT.Copy, scale=2.0, bias=-1.0)\
                        .then_inc(act_sign, 1)

            def scaled_other_part(b, par, before):
                act.wait_ge(sign_used, KC * b + KC)
                wait(act, ht_mm, before)
                nc.scalar.activation(h2[rows_of(par), :].rearrange("p (n c) -> p n c", n=2), dif[rows_of(1 - par)],
                                     ACT.Copy, scale=coef[rows_of(1 - par), bass.ds(b, 1)]).then_inc(dif_sb, 1)

            def evac_h2(o):
                wait(act, h2_stored, 16 * min(o, H2_KEPT) if isinstance(o, int) else 16 * o)
                wait(act, amax_sb, o)
                dst = h2t
                if kept(o, H2_KEPT):
                    if o == PAIRS - 2:
                        act.wait_ge(x1_sb, PAIRS)
                    dst = h2_kept[o - H2_KEPT].rearrange("p (k r) -> p k r", k=KC)
                for half in range(2):
                    act.wait_ge(ht_mm, 2 * o + half + 1)
                    for c in range(4):
                        k = 4 * half + c
                        ins = nc.scalar.activation(dst[:, k, :], turn[half][:, c, :], ACT.Identity,
                                                   bias=bias2[:, k:k + 1])
                ins.then_inc(ht_sb, 1)

            def table_high(i):
                hi, _, stage, _ = staged[i]
                act.wait_ge(table_in[i], 16)
                nc.scalar.activation(hi.rearrange("p k o -> p (k o)"), stage, ACT.Copy).then_inc(table_hi_sb, 1)

            def integer_weights(p, k):
                if isinstance(p, int) and p == PAIRS - 1:
                    act.wait_ge(wq_in, 16)
                    nc.scalar.activation(w_bf[:, k, :], w_i8[:, k, :], ACT.Copy).then_inc(wq_act, 1)

            def weights_high(k):
                act.wait_ge(w_in[k // 4], 16)
                nc.scalar.activation(w_hi[:, k, :], w_stage[k // 4][:, k % 4, :], ACT.Copy).then_inc(w_hi_sb, 1)

            evac_y(0, 0, 0)
            for i in range(4):
                table_high(i)
            yt_high(0)
            squares(0)
            evac_y(1, 0, 1, lin)
            power_high(0)
            for k in range(0, 4):
                weights_high(k)
            act.wait_ge(corr_mm, 1)
            yt_high(1)
            weights_high(4)
            exponentials(0)
            act.wait_ge(w_lo_sb, 4)
            convert(0, 0)
            convert(0, 1)
            weights_high(5)
            weights_high(6)
            act.wait_ge(const_in, 4 * 16)
            act.wait_ge(w_lo_sb, 6)
            xt_high(0, 0)
            weights_high(7)
            squares(1, lin)

            def body(h, q):
                p = 2 * h + q
                m, n, o = p + 2, p + 1, p - 1
                if exists(o):
                    scaled_other_part(2 * p - 1, 1, 2 * p - 2)
                if not is_first(p):
                    convert(p, 1)
                if exists(m):
                    evac_y(m, h + 1, q)
                convert(p, 2)
                if exists(n):
                    power_high(n)
                convert(p, 3)
                if exists(o):
                    evac_h2(o)
                convert(p, 4)
                integer_weights(p, 5)
                scaled_other_part(2 * p, 0, 2 * p)
                convert(p, 5)
                integer_weights(p, 6)
                if exists(n):
                    exponentials(n)
                if exists(m):
                    yt_high(m)
                convert(p, 6)
                integer_weights(p, 7)
                convert(p, 7)
                if exists(n):
                    xt_high(n, 1 - q)
                convert(p, 8)
                if exists(m):
                    squares(m)

            iterations(act, body)
            act.wait_ge(sign_used, KC * B)
            act.wait_ge(ht_mm, 2 * PAIRS - 2)
            for n in range(2):
                nc.scalar.activation(h2[C:P, n * HALF:(n + 1) * HALF], dif[0:C, n, :], ACT.Copy,
                                     scale=coef[0:C, B - 1:B]).then_inc(last_part_sb, 1)
            act.wait_ge(h2_stored, 16 * H2_KEPT)
            act.wait_ge(amax_sb, PAIRS - 1)
            for half in range(2):
                act.wait_ge(ht_mm, 2 * PAIRS - 1 + half)
                for c in range(4):
                    k = 4 * half + c
                    ins = nc.scalar.activation(h2t[:, k, :], turn[half][:, c, :], ACT.Identity, bias=bias2[:, k:k + 1])
                ins.then_inc(last_evac_sb, 1)

            act.wait_ge(scales, 1)
            act.wait_ge(magic_set, 1)

            def round_h2(h, j):
                pair = NB * h + j
                if not kept(pair, H2_KEPT):
                    act.wait_ge(h2_back[j], 16 * h + 16)
                wait(act, q_sb, pair - 1)
                if isinstance(pair, int) and pair == 0:
                    nc.scalar.activation(rnd[:, 0, 0:HALF], h2_of(h, j)[:, 0:HALF], ACT.Identity, bias=magic[:, 0:1],
                                         scale=inv_scale[:, 0:1]).then_inc(first_rnd, 1)
                    nc.scalar.activation(rnd[:, 0, HALF:L], h2_of(h, j)[:, HALF:L], ACT.Identity, bias=magic[:, 0:1],
                                         scale=inv_scale[:, 0:1]).then_inc(rnd_sb, 1)
                    return
                nc.scalar.activation(rnd[:, j % 2, :], h2_of(h, j), ACT.Identity, bias=magic[:, 0:1],
                                     scale=inv_scale[:, 0:1]).then_inc(rnd_sb, 1)

            def evac(pair, j):
                act.wait_ge(mm_done, pair + 1)
                wait(act, scaled_sb, pair - 1)
                nc.scalar.activation(acc[:, j % 2, :].rearrange("p (n c) -> p n c", n=2), prod[j % 2][:], ACT.Copy)\
                    .then_inc(acc_sb, 1)

            def turn_of(h, j):
                round_h2(h, j)
                if isinstance(h, int) and h == 0 and j < 2:
                    return
                evac(NB * h + j - 2, (j - 2) % NB)

            turns(act, turn_of)
            evac(PAIRS - 2, NB - 2)
            act.wait_ge(scaled_sb, PAIRS - 2)
            for n in range(2):
                act.wait_ge(last_mm, n + 1)
                nc.scalar.activation(acc[:, 1, n * HALF:(n + 1) * HALF], prod[1][:, n, :], ACT.Copy)\
                    .then_inc(last_acc, 1)

        @block.vector
        def _(dve):
            def yt_low(m):
                for half in range(2):
                    dve.wait_ge(yt_hi_sb, 2 * m + half + 1)
                    ks = slice(4 * half, 4 * half + 4)
                    nc.vector.tensor_tensor(yt_lo[:, ks, :], turn[half][:], yt_hi[:, ks, :].bitcast(F32),
                                            ALU.subtract).then_inc(yt_lo_sb, 1)

            def power(n):
                dve.wait_ge(sq_sb, n + 1)
                nc.vector.tensor_tensor(sq[:, 1:QT], sq[:, 1:QT], sq[:, QT:2 * QT - 1], ALU.add)
                nc.vector.tensor_tensor(sq[:, 2 * QT:3 * QT], sq[:, 2 * QT:3 * QT], sq[:, 3 * QT:4 * QT], ALU.add)\
                    .then_inc(power_sb, 1)

            def power_low(n):
                dve.wait_ge(pt_hi_sb, n + 1)
                nc.vector.tensor_tensor(pt_lo, att[:, 0, :].rearrange("p (c r) -> p c r", c=4),
                                        pt_hi.bitcast(F32), ALU.subtract).then_inc(pt_lo_sb, 1)

            def correlations(n):
                dve.wait_ge(corr_mm, n + 1)
                nc.vector.scalar_tensor_tensor(out=ce[:], in0=alt[:], scalar=sq[:, 2 * QT - 1:2 * QT],
                                               in1=att[:, 0, 0:TAU], op0=ALU.mult, op1=ALU.add).then_inc(ce_sb, 1)
                dve.wait_ge(ce_sb, n + 1)
                nc.vector.tensor_tensor(corr[:, 0:QT + 1], ce[:, 0:QT + 1], att[:, 1, 0:QT + 1], ALU.add)
                nc.vector.tensor_tensor(corr[:, HALF:HALF + QT + 1], ce[:, 0:QT + 1], att[:, 1, 0:QT + 1],
                                        ALU.subtract).then_inc(corr_sb, 1)

            def top_values(n):
                made = snapped(dve, n + 1)
                keep_apart(dve)
                dve.wait_ge(mirror_sb, made)
                nc.vector.max(top[:], corr[:]).then_inc(top_sb, 1)
                dve.wait_ge(top_sb, 2 * n + 1)
                nc.vector.tensor_scalar(neg_top[:], top[:, 0:1], -1.0, None, ALU.mult).then_inc(top_sb, 1)

            def needed(n):
                nc.vector.tensor_tensor(off_top[:], top[:, 0:1], corr[:, 0:1], ALU.is_gt).then_inc(small_sb, 1)
                dve.wait_ge(small_sb, n + 1)
                dve.wait_ge(exp_sb, n + 1)
                nc.vector.scalar_tensor_tensor(out=need[:], in0=expo[:, 1:2], scalar=0.0, in1=off_top[:],
                                               op0=ALU.is_gt, op1=ALU.add).then_inc(need_sb, 1)

            def shifted_rows(q):
                done = [0]

                def step(ins):
                    done[0] += 1
                    ins.then_inc(general, 1)
                    return done[0]

                step(nc.vector.max_index(lag[:], top[:], corr[:]))
                step(nc.vector.reciprocal(exp_sum[:], exp_sum[:]))
                dve.wait_ge(general, 2)
                step(nc.vector.tensor_scalar(prob[:, 0:TOPK], expo[:, 0:TOPK], exp_sum[:, 0:1], None, ALU.mult))
                for j in range(10):
                    last = step(nc.vector.tensor_scalar(bit_u[:, j, :], lag[:], j, 1, ALU.logical_shift_right,
                                                        ALU.bitwise_and))
                dve.wait_ge(general, last)
                last = step(nc.vector.tensor_copy(bit[:], bit_u[:]))
                dve.wait_ge(general, last)
                base = step(nc.vector.tensor_scalar(bit_not[:], bit[:], -1.0, 1.0, ALU.mult, ALU.add))
                per = 3 * 10 + 1
                with dve.Fori(0, TOPK) as i:
                    src = y[q]
                    for j in range(10):
                        d, dst = 1 << j, (corr, sq)[j % 2]
                        dve.wait_ge(general, per * i + base + 3 * j)
                        nc.vector.tensor_scalar(dst[:], src[:], bit_not[:, j, bass.ds(i, 1)], None, ALU.mult)\
                            .then_inc(general, 1)
                        dve.wait_ge(general, per * i + base + 3 * j + 1)
                        for to, fr in ((slice(0, L - d), slice(d, L)), (slice(L - d, L), slice(0, d))):
                            nc.vector.scalar_tensor_tensor(out=dst[:, to], in0=src[:, fr],
                                                           scalar=bit[:, j, bass.ds(i, 1)], in1=dst[:, to],
                                                           op0=ALU.mult, op1=ALU.add).then_inc(general, 1)
                        src = dst
                    dve.wait_ge(general, per * i + base + 30)
                    nc.vector.scalar_tensor_tensor(out=x[q][:], in0=src[:], scalar=prob[:, bass.ds(i, 1)],
                                                   in1=x[q][:], op0=ALU.mult, op1=ALU.add).then_inc(general, 1)
                dve.wait_ge(general, per * TOPK + base)
                nc.vector.tensor_copy(y[q][:], x[q][:]).then_inc(general, 1)
                dve.wait_ge(general, per * TOPK + base + 1)
                dve.sem_clear(general)

            def make_x1(n, q):
                dve.wait_ge(flag_mm, n + 1)
                nc.vector.tensor_copy(flag[:], att[0:1, 0, 0:1]).then_inc(flag_sb, 1)
                made = snapped(dve, n + 1)
                keep_apart(dve)
                dve.wait_ge(flag_sb, made)
                rows = dve.value_load(flag[0:1, 0:1])
                with dve.If(rows > 0):
                    shifted_rows(q)
                with dve.Else():
                    nc.vector.tensor_tensor(y[q][:], x[q][:], y[q][:], ALU.add).then_inc(general, 1)
                    dve.wait_ge(general, 1)
                    dve.sem_clear(general)
                dve.nop().then_inc(x1_sb, 1)

            def xt_low(n, q):
                for half in range(2):
                    dve.wait_ge(xt_hi_sb, 2 * n + half + 1)
                    ks = slice(4 * half, 4 * half + 4)
                    nc.vector.tensor_tensor(xs[q][:, ks, 1:3, :],
                                            turn[half][:].rearrange("p k (a r) -> p k a r", a=2),
                                            xs[q][:, ks, 0:4:3, :].bitcast(F32), ALU.subtract).then_inc(xt_lo_sb, 1)

            def convert(p, s):
                b, u = unit_of(p, s)
                if isinstance(b, int) and b >= B:
                    return
                for c in DVE_OF[u] if not the_last(b, u) else [KC - 2]:
                    dve.wait_ge(mask_in[u], 16 * b + 16)
                    wait(dve, sign_used, KC * b + c - 3)
                    nc.vector.tensor_scalar(sign[:, c % 4, :], mask_i[:, c, :], 2.0, -1.0, ALU.mult, ALU.add)\
                        .then_inc(dve_sign, 1)

            def both_parts(b, par):
                dve.wait_ge(dif_sb, b + 1)
                r = rows_of(par)
                part = h2[r, :].rearrange("p (n c) -> p n c", n=2)
                nc.vector.scalar_tensor_tensor(out=part, in0=dif[r], scalar=coef[r, bass.ds(b, 1)], in1=part,
                                               op0=ALU.mult, op1=ALU.add).then_inc(s_sb, 1)

            def add_linear(o):
                dve.wait_ge(s_sb, 2 * o + 2)
                dve.wait_ge(lin_mm, o + 1)
                nc.vector.tensor_tensor(h2[:].rearrange("p (n c) -> p n c", n=2), lin[:],
                                        h2[:].rearrange("p (n c) -> p n c", n=2), ALU.add).then_inc(h2_sb, 1)

            def abs_max(o):
                dve.wait_ge(ht_sb, o + 1)
                src = h2_kept[o - H2_KEPT] if kept(o, H2_KEPT) else h2t[:].rearrange("p k r -> p (k r)")
                nc.vector.tensor_reduce(amax_cols[:, bass.ds(o, 1)], src, AX.X,
                                        ALU.max, apply_absolute_value=True).then_inc(amax_sb, 1)

            def table_low(i):
                hi, lo, stage, _ = staged[i]
                dve.wait_ge(table_hi_sb, i + 1)
                nc.vector.tensor_tensor(lo.rearrange("p k o -> p (k o)"), stage,
                                        hi.rearrange("p k o -> p (k o)").bitcast(F32), ALU.subtract)\
                    .then_inc(table_lo_sb, 1)

            def integer_weights(p, k):
                if isinstance(p, int) and p == PAIRS - 1:
                    dve.wait_ge(wq_in, 16)
                    nc.vector.tensor_copy(w_bf[:, k, :], w_i8[:, k, :]).then_inc(wq_dve, 1)

            def weights_low(k):
                dve.wait_ge(w_hi_sb, k + 1)
                nc.vector.tensor_tensor(w_lo[:, k, :], w_stage[k // 4][:, k % 4, :], w_hi[:, k, :].bitcast(F32),
                                        ALU.subtract).then_inc(w_lo_sb, 1)

            nc.vector.memset(warm[:], 1.0).then_inc(warm_sb, 1)
            dve.wait_ge(y_sb, 1)
            first, last = y[0][:, 0:HALF], y[0][:, L - 1:HALF - 1:-1]
            nc.vector.tensor_tensor(fold[:, 0, :], first, last, ALU.add).then_inc(first_folds, 1)
            nc.vector.tensor_tensor(fold[:, 1, :], first, last, ALU.subtract).then_inc(first_folds, 1)
            for i in range(2):
                dve.wait_ge(first_folds, 1 + i)
                first, last = fold[:, i, 0:QT], fold[:, i, HALF - 1:QT - 1:-1]
                nc.vector.tensor_tensor(fold_sum[:, i, :], first, last, ALU.add).then_inc(first_folds, 1)
            for i in range(2):
                dve.wait_ge(first_folds, 3 + i)
                first, last = fold[:, i, 0:QT], fold[:, i, HALF - 1:QT - 1:-1]
                nc.vector.tensor_tensor(first, first, last, ALU.subtract).then_inc(first_folds, 1)
            table_low(0)
            table_low(1)
            yt_low(0)
            table_low(2)
            table_low(3)
            power(0)
            power_low(0)
            weights_low(0)
            weights_low(1)
            dve.wait_ge(const_in, 4 * 16)
            correlations(0)
            weights_low(2)
            yt_low(1)
            weights_low(3)
            top_values(0)
            weights_low(4)
            needed(0)
            convert(0, 0)
            make_x1(0, 0)
            convert(0, 1)
            weights_low(5)
            weights_low(6)
            xt_low(0, 0)
            weights_low(7)

            def body(h, q):
                p = 2 * h + q
                m, n, o = p + 2, p + 1, p - 1
                if exists(n):
                    power(n)
                if exists(o):
                    both_parts(2 * p - 1, 1)
                if not is_first(p):
                    convert(p, 1)
                if exists(o):
                    add_linear(o)
                convert(p, 2)
                if exists(n):
                    power_low(n)
                convert(p, 3)
                integer_weights(p, 0)
                if exists(n):
                    correlations(n)
                convert(p, 4)
                integer_weights(p, 1)
                convert(p, 5)
                integer_weights(p, 2)
                if exists(n):
                    top_values(n)
                both_parts(2 * p, 0)
                if exists(o):
                    abs_max(o)
                if exists(n):
                    needed(n)
                if exists(m):
                    yt_low(m)
                convert(p, 6)
                integer_weights(p, 3)
                if exists(n):
                    make_x1(n, 1 - q)
                convert(p, 7)
                integer_weights(p, 4)
                if exists(n):
                    xt_low(n, 1 - q)
                convert(p, 8)

            iterations(dve, body)
            dve.wait_ge(lin_mm, PAIRS)
            for n in range(2):
                cols = slice(n * HALF, (n + 1) * HALF)
                dve.wait_ge(last_part_sb, n + 1)
                nc.vector.scalar_tensor_tensor(out=h2[C:P, cols], in0=dif[C:P, n, :], scalar=coef[C:P, B - 1:B],
                                               in1=h2[C:P, cols], op0=ALU.mult, op1=ALU.add).then_inc(last_h2_sb, 1)
                dve.wait_ge(last_h2_sb, 2 * n + 1)
                nc.vector.tensor_tensor(h2[:, cols], lin[:, n, :], h2[:, cols], ALU.add).then_inc(last_h2_sb, 1)
            for half in range(2):
                dve.wait_ge(last_evac_sb, half + 1)
                nc.vector.tensor_reduce(amax_cols[:, PAIRS - 1 + half:PAIRS + half],
                                        h2t[:, 4 * half:4 * half + 4, :].rearrange("p k r -> p (k r)"), AX.X,
                                        ALU.max, apply_absolute_value=True).then_inc(amax_sb, 1)

            dve.wait_ge(amax_sb, PAIRS + 1)
            nc.vector.tensor_reduce(amax[:], amax_cols[:], AX.X, ALU.max).then_inc(amax_row_sb, 1)
            dve.wait_ge(amax_all_sb, 1)
            nc.vector.tensor_scalar(zero[:], amax_all[:], 0.0, None, ALU.is_equal)
            nc.vector.tensor_scalar(quot[:], amax_all[:], 1.0 / 127.0, None, ALU.mult).then_inc(sc_sb, 1)
            dve.wait_ge(sc_sb, 1)
            nc.vector.scalar_tensor_tensor(out=rest[:], in0=quot[:], scalar=-128.0, in1=amax_all[:],
                                           op0=ALU.mult, op1=ALU.add).then_inc(sc_sb, 1)
            dve.wait_ge(sc_sb, 2)
            nc.vector.tensor_tensor(rest[:], rest[:], quot[:], ALU.add).then_inc(sc_sb, 1)
            dve.wait_ge(sc_sb, 3)
            nc.vector.scalar_tensor_tensor(out=quot[:], in0=rest[:], scalar=1.0 / 127.0, in1=quot[:],
                                           op0=ALU.mult, op1=ALU.add).then_inc(sc_sb, 1)
            dve.wait_ge(sc_sb, 4)
            nc.vector.tensor_tensor(xsc[:], quot[:], zero[:], ALU.add).then_inc(sc_sb, 1)
            dve.wait_ge(sc_sb, 5)
            nc.vector.reciprocal(inv_scale[:], xsc[:])
            dve.wait_ge(scale_in, 32)
            nc.vector.tensor_tensor(both[:], xsc[:], wsc[:], ALU.mult).then_inc(sc_sb, 1)
            dve.wait_ge(sc_sb, 6)
            nc.vector.tensor_copy(both32[:], both[:]).then_inc(scales, 1)
            dve.wait_ge(scales, 1)

            def quantize(h, j):
                pair = NB * h + j
                if isinstance(pair, int) and pair == 0:
                    for half, (there, low, done) in enumerate([(first_rnd, first_low, first_q), (rnd_sb, low_sb, q_sb)]):
                        part = rnd[:, 0, half * HALF:(half + 1) * HALF]
                        dve.wait_ge(there, 1)
                        nc.vector.tensor_scalar(part, part, MAGIC + 127.0, MAGIC - 127.0, ALU.min, ALU.max)\
                            .then_inc(low, 1)
                        dve.wait_ge(low, 1)
                        nc.vector.tensor_scalar(q8[:, 0, 4 * half:4 * half + 4].rearrange("p k r -> p (k r)"), part,
                                                MAGIC, None, ALU.subtract).then_inc(done, 1)
                    return
                dve.wait_ge(rnd_sb, pair + 1)
                wait(dve, mm_done, pair - 1)
                nc.vector.tensor_scalar(rnd[:, j % 2, :], rnd[:, j % 2, :], MAGIC + 127.0, MAGIC - 127.0,
                                        ALU.min, ALU.max).then_inc(low_sb, 1)
                dve.wait_ge(low_sb, pair + 1)
                nc.vector.tensor_scalar(q8[:, j % 2].rearrange("p k r -> p (k r)"), rnd[:, j % 2, :], MAGIC, None,
                                        ALU.subtract).then_inc(q_sb, 1)

            def finish(h, j, pair):
                dve.wait_ge(acc_sb, pair + 1)
                wait(dve, res_sb, pair - 1)
                nc.vector.tensor_scalar(scaled[:, j % 2, :], acc[:, j % 2, :], both32[:, 0:1], None, ALU.mult)\
                    .then_inc(scaled_sb, 1)
                dve.wait_ge(scaled_sb, pair + 1)
                dve.wait_ge(xb_sb, pair + 1)
                wait(dve, stored[j], 16 * h)
                nc.vector.tensor_tensor(res[:, j, :], scaled[:, j % 2, :], x1_of(h, j), ALU.add).then_inc(res_sb, 1)

            def turn_of(h, j):
                quantize(h, j)
                if isinstance(h, int) and h == 0 and j < 2:
                    return
                finish(h if j >= 2 else h - 1, (j - 2) % NB, NB * h + j - 2)

            turns(dve, turn_of)
            finish(PAIRS // NB - 1, NB - 2, PAIRS - 2)
            dve.wait_ge(res_sb, PAIRS - 2)
            dve.wait_ge(xb_sb, PAIRS)
            dve.wait_ge(stored[NB - 1], 16 * (PAIRS // NB - 1))
            for n in range(2):
                cols = slice(n * HALF, (n + 1) * HALF)
                dve.wait_ge(last_acc, n + 1)
                nc.vector.tensor_scalar(scaled[:, 1, cols], acc[:, 1, cols], both32[:, 0:1], None, ALU.mult)\
                    .then_inc(last_scaled, 1)
                dve.wait_ge(last_scaled, n + 1)
                nc.vector.tensor_tensor(res[:, NB - 1, cols], scaled[:, 1, cols], y[1][:, cols], ALU.add)\
                    .then_inc(last_res, 1)

        @block.gpsimd
        def _(pool):
            nc.gpsimd.memset(cond[:], 0.0).then_inc(pool_const, 1)
            nc.gpsimd.memset(ones[:], 1.0).then_inc(pool_const, 1)
            nc.gpsimd.memset(magic[:], MAGIC).then_inc(magic_set, 1)
            pool.nop().then_inc(started, 1)

            def folds(m, q):
                pool.wait_ge(y_sb, m + 1)
                wait(pool, yt_mm, 2 * m)
                first, last = y[q][:, 0:HALF], y[q][:, L - 1:HALF - 1:-1]
                nc.gpsimd.tensor_tensor(fold[:, 0, :], first, last, ALU.add).then_inc(fold1_sb, 1)
                nc.gpsimd.tensor_tensor(fold[:, 1, :], first, last, ALU.subtract).then_inc(fold1_sb, 1)
                for i in range(2):
                    pool.wait_ge(fold1_sb, 4 * m - 2 + i)
                    first, last = fold[:, i, 0:QT], fold[:, i, HALF - 1:QT - 1:-1]
                    nc.gpsimd.tensor_tensor(fold_sum[:, i, :], first, last, ALU.add).then_inc(fold1_sb, 1)
                pool.wait_ge(fold1_sb, 4 * m)
                for i in range(2):
                    first, last = fold[:, i, 0:QT], fold[:, i, HALF - 1:QT - 1:-1]
                    ins = nc.gpsimd.tensor_tensor(first, first, last, ALU.subtract)
                ins.then_inc(fold2_sb, 1)

            def mirror(n):
                made = snapped(pool, n + 1)
                keep_apart(pool)
                pool.wait_ge(corr_sb, made)
                nc.gpsimd.tensor_copy(corr[:, QT + 1:HALF], corr[:, L - QT - 1:HALF:-1])
                nc.gpsimd.tensor_copy(corr[:, L - QT + 1:L], corr[:, QT - 1:0:-1]).then_inc(mirror_sb, 1)

            def side_by_side(p, q):
                made, used = snapped(pool, 2 * p + 2), snapped(pool, p)
                keep_apart(pool)
                pool.wait_ge(xt_hi_sb, made)
                wait(pool, lin_mm, used)
                for half in range(2):
                    ks = slice(4 * half, 4 * half + 4)
                    nc.gpsimd.tensor_copy(xw[:, ks, :].rearrange("p k (a r) -> p k a r", a=2),
                                          xs[q][:, ks, 0:4:3, :]).then_inc(xw_sb, 1)

            folds(1, 1)
            mirror(0)

            def body(h, q):
                p = 2 * h + q
                side_by_side(p, q)
                if exists(p + 2):
                    folds(p + 2, q)
                if exists(p + 1):
                    mirror(p + 1)

            iterations(pool, body)

            pool.wait_ge(amax_row_sb, 1)
            nc.gpsimd.partition_all_reduce(amax_all[:], amax[:], P, bass.bass_isa.ReduceOp.max).then_inc(amax_all_sb, 1)
            pool.wait_ge(scale_in, 32)

            def add_bias(h, j):
                pair = NB * h + j
                if not kept(pair):
                    pool.wait_ge(x1_back[j], 16 * h + 16)
                nc.gpsimd.tensor_tensor(x1_of(h, j), x1_of(h, j), bias_row[:], ALU.add).then_inc(xb_sb, 1)

            turns(pool, add_bias)



def kernel(x, itok_B_0_15, condB_coeff, mask_Bx4096x4096_ik1, L0_cond_weights, L0_cond2_W, L0_cond2_b,
           L0_ffn_w_int, L0_ffn_w_scale, L0_ffn_bias):
    import concourse.bacc as bacc
    from concourse.bass_utils import run_bass_kernel_spmd as run

    fwd, inv, alt, eye = transform_tables()

    def rows_to_partitions(a):
        return np.ascontiguousarray(a.reshape(KC, P, L).transpose(1, 0, 2))

    arrays = {
        "x": np.ascontiguousarray(x),
        "itok": np.ascontiguousarray(itok_B_0_15),
        "coeff": np.ascontiguousarray(condB_coeff),
        "mask": np.ascontiguousarray(mask_Bx4096x4096_ik1),
        "cond_w": np.ascontiguousarray(L0_cond_weights),
        "w2t": rows_to_partitions(np.asarray(L0_cond2_W).T),
        "b2": np.ascontiguousarray(np.asarray(L0_cond2_b).reshape(KC, P).T),
        "wqt": rows_to_partitions(np.asarray(L0_ffn_w_int).T).view(np.int32),
        "w_scale": np.ascontiguousarray(np.asarray(L0_ffn_w_scale).reshape(1)),
        "bias": np.ascontiguousarray(L0_ffn_bias),
        "t_fwd": fwd, "t_inv": inv, "t_alt": alt, "t_eye": eye,
    }
    nc = bacc.Bacc("TRN2", target_bir_lowering=False, num_devices=1)
    args = [nc.dram_tensor(f"in_{k}", a.shape, mybir.dt.from_np(a.dtype), kind="ExternalInput").ap()
            for k, a in arrays.items()]
    out = nc.dram_tensor("out", (B, C, L), F32, kind="ExternalOutput").ap()
    adaln_attn_ffn(nc, *args, out)
    r = run(nc, [{f"in_{k}": a for k, a in arrays.items()}], core_ids=[0])
    return r.results[0]["out"]
```
